# Optimizing a Trainium2 kernel written in Bass

```python
import numpy as np
import jax
import jax.numpy as jnp

def _softmax(x, axis=-1):
    return jax.nn.softmax(x, axis=axis)

def _gelu(x):
    return jax.nn.gelu(x, approximate=True)

def _silu(x):
    return jax.nn.silu(x)

def _sigmoid(x):
    return jax.nn.sigmoid(x)

def _layernorm(x, axis=-1, eps=1e-05):
    m = jnp.mean(x, axis=axis, keepdims=True)
    v = jnp.var(x, axis=axis, keepdims=True)
    return (x - m) / jnp.sqrt(v + eps)

def _scatter_add(tgt, idx, src, axis=0):
    return tgt.at[idx].add(src)

def _segment_sum(src, seg, n):
    return jax.ops.segment_sum(src, seg, n)
kernel_name = 'mk_xattn_ffn_d4_seqx_r4_0bbb23'

def setup_inputs(seed: int=0):
    np.random.seed(seed)
    _w = jnp.asarray

    def _rec_inputs():
        import jax
        import jax.numpy as jnp
        _rk = jax.random.key(seed)
        x = -0.0002928 + 1 * jax.random.normal(jax.random.fold_in(_rk, 1), (4, 512, 256), jnp.float32)
        _lenS = 512 - jax.random.randint(jax.random.fold_in(_rk, 7), (4,), 0, max(1, 512 // 4) + 1, jnp.int32)
        _lenS2 = 64 - jax.random.randint(jax.random.fold_in(_rk, 8), (4,), 0, max(1, 64 // 4) + 1, jnp.int32)
        _ctx_768P = jax.random.normal(jax.random.fold_in(_rk, 11), (4, 16, 192), jnp.float32)
        _ctx_768c = jax.random.dirichlet(jax.random.fold_in(_rk, 511), 0.3 * jnp.ones((16,), jnp.float32), (4, 64))
        _ctx_768t = jnp.einsum('bsk,bkd->bsd', _ctx_768c, _ctx_768P)
        _ctx_768t = _ctx_768t * jax.lax.rsqrt(jnp.mean(jnp.square(_ctx_768t)) + 1e-12) * 0.953939
        ctx_768 = 2.09791e-05 + 1.00001 * (_ctx_768t + 0.3 * jax.random.normal(jax.random.fold_in(_rk, 611), (4, 64, 192), jnp.float32))
        return (x, ctx_768)
    x, ctx_768 = _rec_inputs()

    def _L0_xattn_setup():
        import jax, jax.numpy as jnp
        import numpy as np
        N_HEADS = 16
        D_HEAD = 64
        key = jax.random.key(seed)
        ks = jax.random.split(key, 7)
        B, SQ, SKV = (2, 512, 512)
        D_MODEL, D_COND, D_ATTN = (256, 192, N_HEADS * D_HEAD)
        return {'x': jax.random.normal(ks[0], (B, SQ, D_MODEL), jnp.float32), 'cond': jax.random.normal(ks[1], (B, SKV, D_COND), jnp.float32), 'w_q': jax.random.normal(ks[2], (D_MODEL, D_ATTN), jnp.float32) * D_MODEL ** (-0.5), 'w_k': jax.random.normal(ks[3], (D_COND, D_ATTN), jnp.float32) * D_COND ** (-0.5), 'w_v': jax.random.normal(ks[4], (D_COND, D_ATTN), jnp.float32) * D_COND ** (-0.5), 'w_out': jax.random.normal(ks[5], (D_ATTN, D_MODEL), jnp.float32) * D_ATTN ** (-0.5), 'b_out': jnp.zeros((D_MODEL,), jnp.float32)}
    _L0_xattn_all = _L0_xattn_setup()
    _L0_xattn_in = {k: v for k, v in _L0_xattn_all.items() if k in ('w_q', 'w_k', 'w_v', 'w_out', 'b_out')}
    del _L0_xattn_all

    def _L0_ffn_setup():
        import jax, jax.numpy as jnp
        import numpy as np
        B, S, D, H = (8, 256, 256, 1024)
        E, R = (3, 8)
        SCALING = 1.0 / R

        def _mole(x, W, b, A, Bm, Rw):
            gates = jax.nn.softmax(jnp.einsum('bsd,de->bse', x, Rw), axis=-1)
            base = jnp.einsum('bsd,dh->bsh', x, W) + b
            z = jnp.einsum('bsd,edr->ebsr', x, A)
            zg = z * jnp.transpose(gates, (2, 0, 1))[..., None]
            lora = jnp.einsum('ebsr,erh->bsh', zg, Bm)
            return base + SCALING * lora
        key = jax.random.key(seed)
        ks = jax.random.split(key, 12)
        s = lambda k, shape, scale: jax.random.normal(k, shape, dtype=jnp.float32) * scale
        return {'x': s(ks[0], (B, S, D), 1.0), 'W1': s(ks[1], (D, H), D ** (-0.5)), 'b1': jnp.zeros((H,), jnp.float32), 'A1': s(ks[2], (E, D, R), D ** (-0.5)), 'B1': s(ks[3], (E, R, H), 0.0) + s(ks[4], (E, R, H), R ** (-0.5)), 'R1': s(ks[5], (D, E), D ** (-0.5)), 'W2': s(ks[6], (H, D), H ** (-0.5)), 'b2': jnp.zeros((D,), jnp.float32), 'A2': s(ks[7], (E, H, R), H ** (-0.5)), 'B2': s(ks[8], (E, R, D), R ** (-0.5)), 'R2': s(ks[9], (H, E), H ** (-0.5))}
    _L0_ffn_all = _L0_ffn_setup()
    _L0_ffn_in = {k: v for k, v in _L0_ffn_all.items() if k in ('W1', 'b1', 'A1', 'B1', 'R1', 'W2', 'b2', 'A2', 'B2', 'R2')}
    del _L0_ffn_all

    def _L1_xattn_setup():
        import jax, jax.numpy as jnp
        import numpy as np
        import math
        N_HEADS = 8
        D_EMBED = 256
        D_CROSS = 192
        D_HEAD = D_EMBED // N_HEADS
        key = jax.random.key(seed)
        ks = jax.random.split(key, 10)
        B, S, SKV = (4, 768, 259)
        s_e = 1.0 / math.sqrt(D_EMBED)
        s_c = 1.0 / math.sqrt(D_CROSS)
        return {'x': jax.random.normal(ks[0], (B, S, D_EMBED), jnp.float32), 'y': jax.random.normal(ks[1], (B, SKV, D_CROSS), jnp.float32), 'Wq': jax.random.normal(ks[2], (D_EMBED, D_EMBED), jnp.float32) * s_e, 'bq': jnp.zeros((D_EMBED,), jnp.float32), 'Wk': jax.random.normal(ks[3], (D_EMBED, D_CROSS), jnp.float32) * s_c, 'bk': jnp.zeros((D_EMBED,), jnp.float32), 'Wv': jax.random.normal(ks[4], (D_EMBED, D_CROSS), jnp.float32) * s_c, 'bv': jnp.zeros((D_EMBED,), jnp.float32), 'Wo': jax.random.normal(ks[5], (D_EMBED, D_EMBED), jnp.float32) * s_e, 'bo': jnp.zeros((D_EMBED,), jnp.float32)}
    _L1_xattn_all = _L1_xattn_setup()
    _L1_xattn_in = {k: v for k, v in _L1_xattn_all.items() if k in ('Wq', 'bq', 'Wk', 'bk', 'Wv', 'bv', 'Wo', 'bo')}
    del _L1_xattn_all

    def _L1_ffn_setup():
        import jax, jax.numpy as jnp
        import numpy as np
        B, S, D_MODEL, D_HIDDEN = (4, 512, 256, 1024)

        def act_quant(x):
            scale = 127.0 / jnp.clip(jnp.max(jnp.abs(x), axis=-1, keepdims=True), 1e-05)
            return jnp.clip(jnp.round(x * scale), -128, 127) / scale

        def weight_quant(w):
            scale = 1.0 / jnp.clip(jnp.mean(jnp.abs(w)), 1e-05)
            return jnp.clip(jnp.round(w * scale), -1, 1) / scale

        def bit_linear(x, w):
            xq = x + jax.lax.stop_gradient(act_quant(x) - x)
            wq = w + jax.lax.stop_gradient(weight_quant(w) - w)
            return jnp.einsum('bsd,hd->bsh', xq, wq)

        def depthwise_conv1d(x_bcl, w, b):
            y = jax.lax.conv_general_dilated(x_bcl, w, window_strides=(1,), padding=[(1, 1)], dimension_numbers=('NCH', 'OIH', 'NCH'), feature_group_count=x_bcl.shape[1])
            return y + b[None, :, None]
        key = jax.random.key(seed)
        ks = jax.random.split(key, 5)
        lim1 = 1.0 / np.sqrt(D_MODEL)
        lim2 = 1.0 / np.sqrt(D_HIDDEN)
        limc = 1.0 / np.sqrt(3.0)
        return {'x': jax.random.normal(ks[0], (B, S, D_MODEL), dtype=jnp.float32), 'w1': jax.random.uniform(ks[1], (D_HIDDEN, D_MODEL), jnp.float32, -lim1, lim1), 'conv_w': jax.random.uniform(ks[2], (D_HIDDEN, 1, 3), jnp.float32, -limc, limc), 'conv_b': jax.random.uniform(ks[3], (D_HIDDEN,), jnp.float32, -limc, limc), 'w2': jax.random.uniform(ks[4], (D_MODEL, D_HIDDEN), jnp.float32, -lim2, lim2)}
    _L1_ffn_all = _L1_ffn_setup()
    _L1_ffn_in = {k: v for k, v in _L1_ffn_all.items() if k in ('w1', 'conv_w', 'conv_b', 'w2')}
    del _L1_ffn_all

    def _L2_xattn_setup():
        import jax, jax.numpy as jnp
        import numpy as np
        IMAGE_DIM = 256
        TEXT_DIM = 192
        NUM_HEADS = 16
        HEAD_DIM = IMAGE_DIM // NUM_HEADS
        key = jax.random.key(seed)
        ks = jax.random.split(key, 14)
        B, N, M = (4, 1024, 128)
        s_img = 1.0 / np.sqrt(IMAGE_DIM)
        s_txt = 1.0 / np.sqrt(TEXT_DIM)
        s_ff = 1.0 / np.sqrt(2 * IMAGE_DIM)
        return {'x': jax.random.normal(ks[0], (B, N, IMAGE_DIM), jnp.float32), 'y': jax.random.normal(ks[1], (B, M, TEXT_DIM), jnp.float32), 'Wq': jax.random.normal(ks[2], (IMAGE_DIM, IMAGE_DIM), jnp.float32) * s_img, 'bq': jax.random.normal(ks[3], (IMAGE_DIM,), jnp.float32) * s_img, 'Wk': jax.random.normal(ks[4], (TEXT_DIM, IMAGE_DIM), jnp.float32) * s_txt, 'bk': jax.random.normal(ks[5], (IMAGE_DIM,), jnp.float32) * s_txt, 'Wv': jax.random.normal(ks[6], (TEXT_DIM, IMAGE_DIM), jnp.float32) * s_txt, 'bv': jax.random.normal(ks[7], (IMAGE_DIM,), jnp.float32) * s_txt, 'W1': jax.random.normal(ks[8], (IMAGE_DIM, 2 * IMAGE_DIM), jnp.float32) * s_img, 'b1': jax.random.normal(ks[9], (2 * IMAGE_DIM,), jnp.float32) * s_img, 'W2': jax.random.normal(ks[10], (2 * IMAGE_DIM, IMAGE_DIM), jnp.float32) * s_ff, 'b2': jax.random.normal(ks[11], (IMAGE_DIM,), jnp.float32) * s_ff}
    _L2_xattn_all = _L2_xattn_setup()
    _L2_xattn_in = {k: v for k, v in _L2_xattn_all.items() if k in ('Wq', 'bq', 'Wk', 'bk', 'Wv', 'bv', 'W1', 'b1', 'W2', 'b2')}
    del _L2_xattn_all

    def _L2_ffn_setup():
        import jax, jax.numpy as jnp
        import numpy as np
        DIM = 256
        DEPTH = 6
        HEADS = 16
        DIM_HEAD = 64
        WINDOW = 64
        INNER = HEADS * DIM_HEAD
        DIM_INNER = int(DIM * 4 * 2 / 3)
        QK_SCALE = 8.0

        def shift_tokens(t):
            a, s = jnp.split(t, 2, -1)
            s = jnp.pad(s, ((0, 0), (1, 0), (0, 0)))[:, :-1]
            return jnp.concatenate([a, s], -1)

        def l2norm(t):
            return t / jnp.maximum(jnp.linalg.norm(t, axis=-1, keepdims=True), 1e-12)

        def rotate_half(x):
            x1, x2 = jnp.split(x, 2, -1)
            return jnp.concatenate([-x2, x1], -1)

        def rotary_tables(n):
            half = jnp.arange(0, DIM_HEAD, 2, dtype=jnp.float32)
            inv_freq = 1.0 / 10000.0 ** (half / DIM_HEAD)
            t = jnp.arange(n, dtype=jnp.float32)
            freqs = t[:, None] * inv_freq[None, :]
            freqs = jnp.concatenate([freqs, freqs], -1)
            base_scale = (half + 0.4 * DIM_HEAD) / (1.4 * DIM_HEAD)
            power = (t - n // 2) / (WINDOW // 2)
            scale = base_scale[None, :] ** power[:, None]
            scale = jnp.concatenate([scale, scale], -1)
            return (freqs, scale)

        def local_attention(q, k, v):
            b, h, n, d = q.shape
            w = WINDOW
            nw = n // w
            bq = q.reshape(b, h, nw, w, d)
            bk = k.reshape(b, h, nw, w, d)
            bv = v.reshape(b, h, nw, w, d)

            def look(t):
                p = jnp.pad(t, ((0, 0), (0, 0), (1, 0), (0, 0), (0, 0)))
                return jnp.concatenate([p[:, :, :nw], p[:, :, 1:]], axis=3)
            bk2, bv2 = (look(bk), look(bv))
            seq = jnp.arange(n).reshape(nw, w)
            seq_p = jnp.pad(seq, ((1, 0), (0, 0)), constant_values=-1)
            jt = jnp.concatenate([seq_p[:nw], seq_p[1:]], axis=1)
            it = seq[:, :, None]
            jb = jt[:, None, :]
            mask = (it < jb) | (it > jb + w) | (jb == -1)
            sim = jnp.einsum('bhwie,bhwje->bhwij', bq, bk2) * QK_SCALE
            sim = jnp.where(mask, -jnp.finfo(sim.dtype).max, sim)
            attn = jax.nn.softmax(sim, -1)
            out = jnp.einsum('bhwij,bhwje->bhwie', attn, bv2)
            return out.reshape(b, h, n, d)

        def attn_layer(x, Wqkv, qs, ksc, Wo):
            b, n, _ = x.shape
            qkv = x @ Wqkv
            q, k, v = jnp.split(qkv, 3, -1)
            sh = lambda t: t.reshape(b, n, HEADS, DIM_HEAD).transpose(0, 2, 1, 3)
            q, k, v = (sh(q), sh(k), sh(v))
            q = l2norm(q) * qs
            k = l2norm(k) * ksc
            freqs, scale = rotary_tables(n)
            cos, sin = (jnp.cos(freqs), jnp.sin(freqs))
            q = q * cos * scale + rotate_half(q) * sin * scale
            inv = 1.0 / scale
            k = k * cos * inv + rotate_half(k) * sin * inv
            out = local_attention(q, k, v)
            out = out.transpose(0, 2, 1, 3).reshape(b, n, INNER)
            return out @ Wo

        def ffn_layer(x, g, bln, W1, b1, W2, b2):
            mu = x.mean(-1, keepdims=True)
            var = ((x - mu) ** 2).mean(-1, keepdims=True)
            xn = (x - mu) / jnp.sqrt(var + 1e-05) * g + bln
            hg = xn @ W1 + b1
            a, gate = jnp.split(hg, 2, -1)
            return a * jax.nn.gelu(gate, approximate=False) @ W2 + b2
        key = jax.random.key(seed)
        ks = jax.random.split(key, 8)
        B, N = (2, 512)
        init = lambda k, shape: jax.random.normal(k, shape, jnp.float32) * 0.02
        return {'x': jax.random.normal(ks[0], (B, N, DIM), jnp.float32), 'Wqkv': init(ks[1], (DEPTH, DIM, 3 * INNER)), 'q_scale': jnp.ones((DEPTH, DIM_HEAD), jnp.float32), 'k_scale': jnp.ones((DEPTH, DIM_HEAD), jnp.float32), 'Wo': init(ks[2], (DEPTH, INNER, DIM)), 'ln_g': jnp.ones((DEPTH, DIM), jnp.float32), 'ln_b': jnp.zeros((DEPTH, DIM), jnp.float32), 'W1': init(ks[3], (DEPTH, DIM, 2 * DIM_INNER)), 'b1': jnp.zeros((DEPTH, 2 * DIM_INNER), jnp.float32), 'W2': init(ks[4], (DEPTH, DIM_INNER, DIM)), 'b2': jnp.zeros((DEPTH, DIM), jnp.float32)}
    _L2_ffn_all = _L2_ffn_setup()
    _L2_ffn_in = {k: v for k, v in _L2_ffn_all.items() if k in ('Wqkv', 'q_scale', 'k_scale', 'Wo', 'ln_g', 'ln_b', 'W1', 'b1', 'W2', 'b2')}
    del _L2_ffn_all

    def _L3_xattn_setup():
        import jax, jax.numpy as jnp
        import numpy as np
        B, LQ, LKV = (4, 128, 512)
        DQ, DKV, H = (256, 192, 16)
        HD = DQ // H
        key = jax.random.key(seed)
        ks = jax.random.split(key, 12)
        s_q = 1.0 / np.sqrt(DQ)
        s_kv = 1.0 / np.sqrt(DKV)
        return {'q': jax.random.normal(ks[0], (B, LQ, DQ), jnp.float32), 'kv': jax.random.normal(ks[1], (B, LKV, DKV), jnp.float32), 'Wq': jax.random.normal(ks[2], (DQ, DQ), jnp.float32) * s_q, 'bq': jnp.zeros((DQ,), jnp.float32), 'Wk': jax.random.normal(ks[3], (DKV, DQ), jnp.float32) * s_kv, 'bk': jnp.zeros((DQ,), jnp.float32), 'Wv': jax.random.normal(ks[4], (DKV, DQ), jnp.float32) * s_kv, 'bv': jnp.zeros((DQ,), jnp.float32), 'Wo': jax.random.normal(ks[5], (DQ, DQ), jnp.float32) * s_q, 'bo': jnp.zeros((DQ,), jnp.float32), 'scale': jnp.ones((1,), jnp.float32) * DQ ** (-0.5)}
    _L3_xattn_all = _L3_xattn_setup()
    _L3_xattn_in = {k: v for k, v in _L3_xattn_all.items() if k in ('Wq', 'bq', 'Wk', 'bk', 'Wv', 'bv', 'Wo', 'bo', 'scale')}
    del _L3_xattn_all

    def _L3_ffn_setup():
        import jax, jax.numpy as jnp
        import numpy as np
        E = 8
        K = 2
        key = jax.random.key(seed)
        ks = jax.random.split(key, 8)
        B, T, d = (4, 512, 256)
        h = 4 * d // E
        s = 0.02
        X = jax.random.normal(ks[0], (B, T, d), jnp.float32)
        routing_W = jax.random.normal(ks[1], (E, d), jnp.float32) * s
        expert_bias = jnp.zeros((E,), jnp.float32)
        sW1 = jax.random.normal(ks[2], (d, h), jnp.float32) * s
        sb1 = jnp.zeros((h,), jnp.float32)
        sW2 = jax.random.normal(ks[3], (h, d), jnp.float32) * s
        sb2 = jnp.zeros((d,), jnp.float32)
        rW1 = jax.random.normal(ks[4], (E, d, h), jnp.float32) * s
        rb1 = jnp.zeros((E, h), jnp.float32)
        rW2 = jax.random.normal(ks[5], (E, h, d), jnp.float32) * s
        rb2 = jnp.zeros((E, d), jnp.float32)
        return dict(X=X, routing_W=routing_W, expert_bias=expert_bias, sW1=sW1, sb1=sb1, sW2=sW2, sb2=sb2, rW1=rW1, rb1=rb1, rW2=rW2, rb2=rb2)
    _L3_ffn_all = _L3_ffn_setup()
    _L3_ffn_in = {k: v for k, v in _L3_ffn_all.items() if k in ('routing_W', 'expert_bias', 'sW1', 'sb1', 'sW2', 'sb2', 'rW1', 'rb1', 'rW2', 'rb2')}
    del _L3_ffn_all
    return {'x': x, 'ctx_768': ctx_768, 'L0_xattn_w_q': _L0_xattn_in['w_q'], 'L0_xattn_w_k': _L0_xattn_in['w_k'], 'L0_xattn_w_v': _L0_xattn_in['w_v'], 'L0_xattn_w_out': _L0_xattn_in['w_out'], 'L0_xattn_b_out': _L0_xattn_in['b_out'], 'L0_ffn_W1': _L0_ffn_in['W1'], 'L0_ffn_b1': _L0_ffn_in['b1'], 'L0_ffn_A1': _L0_ffn_in['A1'], 'L0_ffn_B1': _L0_ffn_in['B1'], 'L0_ffn_R1': _L0_ffn_in['R1'], 'L0_ffn_W2': _L0_ffn_in['W2'], 'L0_ffn_b2': _L0_ffn_in['b2'], 'L0_ffn_A2': _L0_ffn_in['A2'], 'L0_ffn_B2': _L0_ffn_in['B2'], 'L0_ffn_R2': _L0_ffn_in['R2'], 'L1_xattn_Wq': _L1_xattn_in['Wq'], 'L1_xattn_bq': _L1_xattn_in['bq'], 'L1_xattn_Wk': _L1_xattn_in['Wk'], 'L1_xattn_bk': _L1_xattn_in['bk'], 'L1_xattn_Wv': _L1_xattn_in['Wv'], 'L1_xattn_bv': _L1_xattn_in['bv'], 'L1_xattn_Wo': _L1_xattn_in['Wo'], 'L1_xattn_bo': _L1_xattn_in['bo'], 'L1_ffn_w1': _L1_ffn_in['w1'], 'L1_ffn_conv_w': _L1_ffn_in['conv_w'], 'L1_ffn_conv_b': _L1_ffn_in['conv_b'], 'L1_ffn_w2': _L1_ffn_in['w2'], 'L2_xattn_Wq': _L2_xattn_in['Wq'], 'L2_xattn_bq': _L2_xattn_in['bq'], 'L2_xattn_Wk': _L2_xattn_in['Wk'], 'L2_xattn_bk': _L2_xattn_in['bk'], 'L2_xattn_Wv': _L2_xattn_in['Wv'], 'L2_xattn_bv': _L2_xattn_in['bv'], 'L2_xattn_W1': _L2_xattn_in['W1'], 'L2_xattn_b1': _L2_xattn_in['b1'], 'L2_xattn_W2': _L2_xattn_in['W2'], 'L2_xattn_b2': _L2_xattn_in['b2'], 'L2_ffn_Wqkv': _L2_ffn_in['Wqkv'], 'L2_ffn_q_scale': _L2_ffn_in['q_scale'], 'L2_ffn_k_scale': _L2_ffn_in['k_scale'], 'L2_ffn_Wo': _L2_ffn_in['Wo'], 'L2_ffn_ln_g': _L2_ffn_in['ln_g'], 'L2_ffn_ln_b': _L2_ffn_in['ln_b'], 'L2_ffn_W1': _L2_ffn_in['W1'], 'L2_ffn_b1': _L2_ffn_in['b1'], 'L2_ffn_W2': _L2_ffn_in['W2'], 'L2_ffn_b2': _L2_ffn_in['b2'], 'L3_xattn_Wq': _L3_xattn_in['Wq'], 'L3_xattn_bq': _L3_xattn_in['bq'], 'L3_xattn_Wk': _L3_xattn_in['Wk'], 'L3_xattn_bk': _L3_xattn_in['bk'], 'L3_xattn_Wv': _L3_xattn_in['Wv'], 'L3_xattn_bv': _L3_xattn_in['bv'], 'L3_xattn_Wo': _L3_xattn_in['Wo'], 'L3_xattn_bo': _L3_xattn_in['bo'], 'L3_xattn_scale': _L3_xattn_in['scale'], 'L3_ffn_routing_W': _L3_ffn_in['routing_W'], 'L3_ffn_expert_bias': _L3_ffn_in['expert_bias'], 'L3_ffn_sW1': _L3_ffn_in['sW1'], 'L3_ffn_sb1': _L3_ffn_in['sb1'], 'L3_ffn_sW2': _L3_ffn_in['sW2'], 'L3_ffn_sb2': _L3_ffn_in['sb2'], 'L3_ffn_rW1': _L3_ffn_in['rW1'], 'L3_ffn_rb1': _L3_ffn_in['rb1'], 'L3_ffn_rW2': _L3_ffn_in['rW2'], 'L3_ffn_rb2': _L3_ffn_in['rb2']}

def reference(x, ctx_768, L0_xattn_w_q, L0_xattn_w_k, L0_xattn_w_v, L0_xattn_w_out, L0_xattn_b_out, L0_ffn_W1, L0_ffn_b1, L0_ffn_A1, L0_ffn_B1, L0_ffn_R1, L0_ffn_W2, L0_ffn_b2, L0_ffn_A2, L0_ffn_B2, L0_ffn_R2, L1_xattn_Wq, L1_xattn_bq, L1_xattn_Wk, L1_xattn_bk, L1_xattn_Wv, L1_xattn_bv, L1_xattn_Wo, L1_xattn_bo, L1_ffn_w1, L1_ffn_conv_w, L1_ffn_conv_b, L1_ffn_w2, L2_xattn_Wq, L2_xattn_bq, L2_xattn_Wk, L2_xattn_bk, L2_xattn_Wv, L2_xattn_bv, L2_xattn_W1, L2_xattn_b1, L2_xattn_W2, L2_xattn_b2, L2_ffn_Wqkv, L2_ffn_q_scale, L2_ffn_k_scale, L2_ffn_Wo, L2_ffn_ln_g, L2_ffn_ln_b, L2_ffn_W1, L2_ffn_b1, L2_ffn_W2, L2_ffn_b2, L3_xattn_Wq, L3_xattn_bq, L3_xattn_Wk, L3_xattn_bk, L3_xattn_Wv, L3_xattn_bv, L3_xattn_Wo, L3_xattn_bo, L3_xattn_scale, L3_ffn_routing_W, L3_ffn_expert_bias, L3_ffn_sW1, L3_ffn_sb1, L3_ffn_sW2, L3_ffn_sb2, L3_ffn_rW1, L3_ffn_rb1, L3_ffn_rW2, L3_ffn_rb2):
    import jax
    import jax.numpy as jnp

    def _L0_xattn_ref(x, cond, w_q, w_k, w_v, w_out, b_out):
        import jax, jax.numpy as jnp
        import numpy as np
        N_HEADS = 16
        D_HEAD = 64
        B, SQ, _ = x.shape
        SKV = cond.shape[1]
        scale = D_HEAD ** (-0.5)
        q = (x @ w_q).reshape(B, SQ, N_HEADS, D_HEAD)
        k = (cond @ w_k).reshape(B, SKV, N_HEADS, D_HEAD)
        v = (cond @ w_v).reshape(B, SKV, N_HEADS, D_HEAD)
        attn = jnp.einsum('bqhd,bkhd->bhqk', q, k) * scale
        attn = jax.nn.softmax(attn, axis=-1)
        out = jnp.einsum('bhqk,bkhd->bqhd', attn, v).reshape(B, SQ, N_HEADS * D_HEAD)
        return out @ w_out + b_out

    def _L0_ffn_ref(x, W1, b1, A1, B1, R1, W2, b2, A2, B2, R2):
        import jax, jax.numpy as jnp
        import numpy as np
        B, S, D, H = (8, 256, 256, 1024)
        E, R = (3, 8)
        SCALING = 1.0 / R

        def _mole(x, W, b, A, Bm, Rw):
            gates = jax.nn.softmax(jnp.einsum('bsd,de->bse', x, Rw), axis=-1)
            base = jnp.einsum('bsd,dh->bsh', x, W) + b
            z = jnp.einsum('bsd,edr->ebsr', x, A)
            zg = z * jnp.transpose(gates, (2, 0, 1))[..., None]
            lora = jnp.einsum('ebsr,erh->bsh', zg, Bm)
            return base + SCALING * lora
        h = _mole(x, W1, b1, A1, B1, R1)
        h = jax.nn.relu(h)
        return _mole(h, W2, b2, A2, B2, R2)

    def _L1_xattn_ref(x, y, Wq, bq, Wk, bk, Wv, bv, Wo, bo):
        import jax, jax.numpy as jnp
        import numpy as np
        import math
        N_HEADS = 8
        D_EMBED = 256
        D_CROSS = 192
        D_HEAD = D_EMBED // N_HEADS
        B, S, _ = x.shape
        SKV = y.shape[1]
        q = x @ Wq.T + bq
        k = y @ Wk.T + bk
        v = y @ Wv.T + bv
        q = q.reshape(B, S, N_HEADS, D_HEAD).transpose(0, 2, 1, 3)
        k = k.reshape(B, SKV, N_HEADS, D_HEAD).transpose(0, 2, 1, 3)
        v = v.reshape(B, SKV, N_HEADS, D_HEAD).transpose(0, 2, 1, 3)
        scores = jnp.einsum('bhqd,bhkd->bhqk', q, k) / math.sqrt(D_HEAD)
        attn = jax.nn.softmax(scores, axis=-1)
        out = jnp.einsum('bhqk,bhkd->bhqd', attn, v)
        out = out.transpose(0, 2, 1, 3).reshape(B, S, D_EMBED)
        return out @ Wo.T + bo

    def _L1_ffn_ref(x, w1, conv_w, conv_b, w2):
        import jax, jax.numpy as jnp
        import numpy as np
        B, S, D_MODEL, D_HIDDEN = (4, 512, 256, 1024)

        def act_quant(x):
            scale = 127.0 / jnp.clip(jnp.max(jnp.abs(x), axis=-1, keepdims=True), 1e-05)
            return jnp.clip(jnp.round(x * scale), -128, 127) / scale

        def weight_quant(w):
            scale = 1.0 / jnp.clip(jnp.mean(jnp.abs(w)), 1e-05)
            return jnp.clip(jnp.round(w * scale), -1, 1) / scale

        def bit_linear(x, w):
            xq = x + jax.lax.stop_gradient(act_quant(x) - x)
            wq = w + jax.lax.stop_gradient(weight_quant(w) - w)
            return jnp.einsum('bsd,hd->bsh', xq, wq)

        def depthwise_conv1d(x_bcl, w, b):
            y = jax.lax.conv_general_dilated(x_bcl, w, window_strides=(1,), padding=[(1, 1)], dimension_numbers=('NCH', 'OIH', 'NCH'), feature_group_count=x_bcl.shape[1])
            return y + b[None, :, None]
        h = bit_linear(x, w1)
        h = depthwise_conv1d(h.transpose(0, 2, 1), conv_w, conv_b)
        h = h.transpose(0, 2, 1)
        h = jax.nn.silu(h)
        return bit_linear(h, w2)

    def _L2_xattn_ref(x, y, Wq, bq, Wk, bk, Wv, bv, W1, b1, W2, b2):
        import jax, jax.numpy as jnp
        import numpy as np
        IMAGE_DIM = 256
        TEXT_DIM = 192
        NUM_HEADS = 16
        HEAD_DIM = IMAGE_DIM // NUM_HEADS
        B, N, _ = x.shape
        M = y.shape[1]
        q = (x @ Wq + bq).reshape(B, N, NUM_HEADS, HEAD_DIM)
        k = (y @ Wk + bk).reshape(B, M, NUM_HEADS, HEAD_DIM)
        v = (y @ Wv + bv).reshape(B, M, NUM_HEADS, HEAD_DIM)
        scale = 1.0 / np.sqrt(HEAD_DIM)
        scores = jnp.einsum('bnhd,bmhd->bhnm', q, k) * scale
        attn = jax.nn.softmax(scores, axis=-1)
        out = jnp.einsum('bhnm,bmhd->bnhd', attn, v).reshape(B, N, IMAGE_DIM)
        h = jax.nn.relu(out @ W1 + b1)
        return h @ W2 + b2

    def _L2_ffn_ref(x, Wqkv, q_scale, k_scale, Wo, ln_g, ln_b, W1, b1, W2, b2):
        import jax, jax.numpy as jnp
        import numpy as np
        DIM = 256
        DEPTH = 6
        HEADS = 16
        DIM_HEAD = 64
        WINDOW = 64
        INNER = HEADS * DIM_HEAD
        DIM_INNER = int(DIM * 4 * 2 / 3)
        QK_SCALE = 8.0

        def shift_tokens(t):
            a, s = jnp.split(t, 2, -1)
            s = jnp.pad(s, ((0, 0), (1, 0), (0, 0)))[:, :-1]
            return jnp.concatenate([a, s], -1)

        def l2norm(t):
            return t / jnp.maximum(jnp.linalg.norm(t, axis=-1, keepdims=True), 1e-12)

        def rotate_half(x):
            x1, x2 = jnp.split(x, 2, -1)
            return jnp.concatenate([-x2, x1], -1)

        def rotary_tables(n):
            half = jnp.arange(0, DIM_HEAD, 2, dtype=jnp.float32)
            inv_freq = 1.0 / 10000.0 ** (half / DIM_HEAD)
            t = jnp.arange(n, dtype=jnp.float32)
            freqs = t[:, None] * inv_freq[None, :]
            freqs = jnp.concatenate([freqs, freqs], -1)
            base_scale = (half + 0.4 * DIM_HEAD) / (1.4 * DIM_HEAD)
            power = (t - n // 2) / (WINDOW // 2)
            scale = base_scale[None, :] ** power[:, None]
            scale = jnp.concatenate([scale, scale], -1)
            return (freqs, scale)

        def local_attention(q, k, v):
            b, h, n, d = q.shape
            w = WINDOW
            nw = n // w
            bq = q.reshape(b, h, nw, w, d)
            bk = k.reshape(b, h, nw, w, d)
            bv = v.reshape(b, h, nw, w, d)

            def look(t):
                p = jnp.pad(t, ((0, 0), (0, 0), (1, 0), (0, 0), (0, 0)))
                return jnp.concatenate([p[:, :, :nw], p[:, :, 1:]], axis=3)
            bk2, bv2 = (look(bk), look(bv))
            seq = jnp.arange(n).reshape(nw, w)
            seq_p = jnp.pad(seq, ((1, 0), (0, 0)), constant_values=-1)
            jt = jnp.concatenate([seq_p[:nw], seq_p[1:]], axis=1)
            it = seq[:, :, None]
            jb = jt[:, None, :]
            mask = (it < jb) | (it > jb + w) | (jb == -1)
            sim = jnp.einsum('bhwie,bhwje->bhwij', bq, bk2) * QK_SCALE
            sim = jnp.where(mask, -jnp.finfo(sim.dtype).max, sim)
            attn = jax.nn.softmax(sim, -1)
            out = jnp.einsum('bhwij,bhwje->bhwie', attn, bv2)
            return out.reshape(b, h, n, d)

        def attn_layer(x, Wqkv, qs, ksc, Wo):
            b, n, _ = x.shape
            qkv = x @ Wqkv
            q, k, v = jnp.split(qkv, 3, -1)
            sh = lambda t: t.reshape(b, n, HEADS, DIM_HEAD).transpose(0, 2, 1, 3)
            q, k, v = (sh(q), sh(k), sh(v))
            q = l2norm(q) * qs
            k = l2norm(k) * ksc
            freqs, scale = rotary_tables(n)
            cos, sin = (jnp.cos(freqs), jnp.sin(freqs))
            q = q * cos * scale + rotate_half(q) * sin * scale
            inv = 1.0 / scale
            k = k * cos * inv + rotate_half(k) * sin * inv
            out = local_attention(q, k, v)
            out = out.transpose(0, 2, 1, 3).reshape(b, n, INNER)
            return out @ Wo

        def ffn_layer(x, g, bln, W1, b1, W2, b2):
            mu = x.mean(-1, keepdims=True)
            var = ((x - mu) ** 2).mean(-1, keepdims=True)
            xn = (x - mu) / jnp.sqrt(var + 1e-05) * g + bln
            hg = xn @ W1 + b1
            a, gate = jnp.split(hg, 2, -1)
            return a * jax.nn.gelu(gate, approximate=False) @ W2 + b2
        for i in range(DEPTH):
            x = attn_layer(shift_tokens(x), Wqkv[i], q_scale[i], k_scale[i], Wo[i]) + x
            x = ffn_layer(shift_tokens(x), ln_g[i], ln_b[i], W1[i], b1[i], W2[i], b2[i]) + x
        return x

    def _L3_xattn_ref(q, kv, Wq, bq, Wk, bk, Wv, bv, Wo, bo, scale):
        import jax, jax.numpy as jnp
        import numpy as np
        B, LQ, LKV = (4, 128, 512)
        DQ, DKV, H = (256, 192, 16)
        HD = DQ // H
        b, lq, _ = q.shape
        lkv = kv.shape[1]
        qh = (q @ Wq + bq).reshape(b, lq, H, HD).transpose(0, 2, 1, 3)
        kh = (kv @ Wk + bk).reshape(b, lkv, H, HD).transpose(0, 2, 1, 3)
        vh = (kv @ Wv + bv).reshape(b, lkv, H, HD).transpose(0, 2, 1, 3)
        scores = jnp.einsum('bhqd,bhkd->bhqk', qh, kh) * scale[0]
        attn = jax.nn.softmax(scores, axis=-1)
        out = jnp.einsum('bhqk,bhkd->bhqd', attn, vh)
        out = out.transpose(0, 2, 1, 3).reshape(b, lq, DQ)
        return out @ Wo + bo

    def _L3_ffn_ref(X, routing_W, expert_bias, sW1, sb1, sW2, sb2, rW1, rb1, rW2, rb2):
        import jax, jax.numpy as jnp
        import numpy as np
        E = 8
        K = 2
        B, T, d = X.shape
        shared = jax.nn.silu(X @ sW1 + sb1) @ sW2 + sb2
        logits = jnp.einsum('btd,ed->bte', X, routing_W) + expert_bias
        activation = jnp.sqrt(jax.nn.softplus(logits))
        top_vals, top_idx = jax.lax.top_k(activation, K)
        combine = jnp.sum(jax.nn.one_hot(top_idx, E, dtype=X.dtype) * top_vals[..., None], axis=-2)
        Xf = X.reshape(-1, d)
        cf = combine.reshape(-1, E)
        hdn = jax.nn.silu(jnp.einsum('nd,edh->enh', Xf, rW1) + rb1[:, None, :])
        y = jnp.einsum('enh,ehd->end', hdn, rW2) + rb2[:, None, :]
        routed = jnp.einsum('ne,end->nd', cf, y).reshape(B, T, d)
        return shared + routed
    x = x + _L0_xattn_ref(_layernorm(x, axis=-1), ctx_768, L0_xattn_w_q, L0_xattn_w_k, L0_xattn_w_v, L0_xattn_w_out, L0_xattn_b_out)
    x = x + _L0_ffn_ref(_layernorm(x, axis=-1), L0_ffn_W1, L0_ffn_b1, L0_ffn_A1, L0_ffn_B1, L0_ffn_R1, L0_ffn_W2, L0_ffn_b2, L0_ffn_A2, L0_ffn_B2, L0_ffn_R2)
    x = x + _L1_xattn_ref(_layernorm(x, axis=-1), ctx_768, L1_xattn_Wq, L1_xattn_bq, L1_xattn_Wk, L1_xattn_bk, L1_xattn_Wv, L1_xattn_bv, L1_xattn_Wo, L1_xattn_bo)
    x = x + _L1_ffn_ref(_layernorm(x, axis=-1), L1_ffn_w1, L1_ffn_conv_w, L1_ffn_conv_b, L1_ffn_w2)
    x = x + _L2_xattn_ref(_layernorm(x, axis=-1), ctx_768, L2_xattn_Wq, L2_xattn_bq, L2_xattn_Wk, L2_xattn_bk, L2_xattn_Wv, L2_xattn_bv, L2_xattn_W1, L2_xattn_b1, L2_xattn_W2, L2_xattn_b2)
    x = x + _L2_ffn_ref(_layernorm(x, axis=-1), L2_ffn_Wqkv, L2_ffn_q_scale, L2_ffn_k_scale, L2_ffn_Wo, L2_ffn_ln_g, L2_ffn_ln_b, L2_ffn_W1, L2_ffn_b1, L2_ffn_W2, L2_ffn_b2)
    x = x + _L3_xattn_ref(_layernorm(x, axis=-1), ctx_768, L3_xattn_Wq, L3_xattn_bq, L3_xattn_Wk, L3_xattn_bk, L3_xattn_Wv, L3_xattn_bv, L3_xattn_Wo, L3_xattn_bo, L3_xattn_scale)
    x = x + _L3_ffn_ref(_layernorm(x, axis=-1), L3_ffn_routing_W, L3_ffn_expert_bias, L3_ffn_sW1, L3_ffn_sb1, L3_ffn_sW2, L3_ffn_sb2, L3_ffn_rW1, L3_ffn_rb1, L3_ffn_rW2, L3_ffn_rb2)
    return x

_drawn_inputs = setup_inputs


def setup_inputs(seed=0):
    import zlib

    import numpy as np

    out = dict(_drawn_inputs(seed))
    spreads = {'L0_xattn_b_out': (0.0, 0.1),
     'L0_ffn_b1': (0.0, 0.1),
     'L0_ffn_b2': (0.0, 0.1),
     'L1_xattn_bq': (0.0, 0.478),
     'L1_xattn_bk': (0.0, 0.8),
     'L1_xattn_bv': (0.0, 0.1),
     'L1_xattn_bo': (0.0, 0.1),
     'L2_ffn_q_scale': (1.0, 0.6),
     'L2_ffn_k_scale': (1.0, 0.6),
     'L2_ffn_ln_g': (1.0, 0.6),
     'L2_ffn_ln_b': (0.0, 0.8),
     'L2_ffn_b1': (0.0, 0.537),
     'L2_ffn_b2': (0.0, 0.1),
     'L3_xattn_bq': (0.0, 0.8),
     'L3_xattn_bk': (0.0, 0.8),
     'L3_xattn_bv': (0.0, 0.1),
     'L3_xattn_bo': (0.0, 0.1),
     'L3_ffn_expert_bias': (0.0, 0.1),
     'L3_ffn_sb1': (0.0, 0.8),
     'L3_ffn_sb2': (0.0, 0.1),
     'L3_ffn_rb1': (0.0, 0.8),
     'L3_ffn_rb2': (0.0, 0.1)}
    factors = {'L2_xattn_bq': 7.682,
     'L2_xattn_bk': 8.0,
     'L3_xattn_Wq': 2.716,
     'L3_ffn_sW1': 4.114,
     'L3_ffn_sW2': 3.694,
     'L3_ffn_rW1': 2.932,
     'L3_ffn_rW2': 2.743}
    for name, (base, spread) in spreads.items():
        noise = np.random.default_rng([zlib.crc32(name.encode()), seed]).standard_normal(out[name].shape)
        drawn = base * np.exp(spread * noise) if base else spread * noise
        out[name] = jnp.asarray(drawn.astype(out[name].dtype))
    for name, factor in factors.items():
        out[name] = (out[name] * factor).astype(out[name].dtype)
    return out
```

```python
from contextlib import ExitStack

import concourse.bass as bass
from concourse import mybir

F32 = mybir.dt.float32
BF16 = mybir.dt.bfloat16
F32R = mybir.dt.float32r
ALU = mybir.AluOpType
ACT = mybir.ActivationFunctionType
AX = mybir.AxisListType

P = 128
B = 4
T = 512
NT = T // P
D = 256
KD = D // P
KEYS = 64
DC = 192
CK = ((0, 128), (1, 64))
EPS = 1e-5
BANK = 512




def upper(x):
    names = "abcd"[:len(x.shape) - 2]
    last = " ".join(names)
    return x.bitcast(BF16).rearrange(f"p {last} (n half) -> p {last} n half", half=2)[(slice(None),) * (len(x.shape)) + (1,)]


def split_matmul(pe, out, weights, moving, start, stop):
    pe.matmul(out, weights[0].bitcast(F32R), moving[0].bitcast(F32R), start=start, stop=False)
    pe.matmul(out, upper(weights[0]), moving[1], start=False, stop=False)
    return pe.matmul(out, weights[1], upper(moving[0]), start=False, stop=stop)


class Signal:

    def __init__(self, sem, per, ahead=0):
        self.sem, self.per, self.ahead = sem, per, ahead

    def at(self, it, k=0):
        return it * self.per + k + self.ahead

    def raise_ahead(self, eng):
        assert self.ahead == 1
        eng.sem_inc(self.sem, 1)


class Chain:

    def __init__(self, eng, steps, it):
        self.eng, self.steps, self.it, self.n = eng, steps, it, 0

    def __call__(self, ins):
        self.n += 1
        ins.then_inc(self.steps.sem, 1)
        self.eng.wait_ge(self.steps.sem, self.steps.at(self.it, self.n))

    def end(self):
        assert self.n == self.steps.per, (self.n, self.steps.per)


class Section:

    def __init__(self, nc, ctx, name):
        self.nc, self.ctx, self.name = nc, ctx, name
        self.numbers = []

    def sb(self, name, shape, dt=F32):
        return self.ctx.enter_context(self.nc.sbuf_tensor(f"{self.name}_{name}", shape, dt))

    def sig(self, name, per=1, ahead=0):
        sem = self.ctx.enter_context(self.nc.semaphore(f"{self.name}_{name}"))
        self.numbers.append(sem.num)
        return Signal(sem, per, ahead)

    def block(self):
        def clear():
            self.nc.gpsimd.sem_clear(range(min(self.numbers), max(self.numbers) + 1))
            self.nc.all_engine_barrier()

        self.ctx.callback(clear)
        return self.ctx.enter_context(self.nc.Block())




class LayerNorm:

    def __init__(self, s, K, ps):
        self.K, self.ps = K, ps
        self.xc = s.sb("centered", [P, KD, T])
        self.sq = s.sb("squares", [P, KD, T])
        self.rstd = s.sb("rstd", [P, T])
        self.xn = self.sq
        self.mean_ready = s.sig("mean_ready")
        self.centered_ready = s.sig("centered_ready")
        self.squares_ready = s.sig("squares_ready")
        self.var_ready = s.sig("var_ready")
        self.log_ready = s.sig("log_ready")
        self.rstd_ready = s.sig("rstd_ready")
        self.xn_ready = s.sig("xn_ready")

    def pe_mean(self, pe, x_of):
        for k in range(KD):
            ins = pe.matmul(self.ps[:, 0, :], self.K.mean[:, :], x_of(k), start=k == 0, stop=k == KD - 1)
        ins.then_inc(self.mean_ready.sem, 1)

    def pe_var(self, pe, it):
        pe.wait_ge(self.squares_ready.sem, self.squares_ready.at(it, 1))
        for k in range(KD):
            ins = pe.matmul(self.ps[:, 1, :], self.K.mean[:, :], self.sq[:, k, :], start=k == 0, stop=k == KD - 1)
        ins.then_inc(self.var_ready.sem, 1)

    def dve_center(self, dve, it, x_all_of):
        dve.wait_ge(self.mean_ready.sem, self.mean_ready.at(it, 1))
        mean = self.ps[:, 0:1, :].broadcast_to([P, KD, T])
        dve.tensor_tensor(self.xc[:, :, :], x_all_of, mean, ALU.subtract).then_inc(self.centered_ready.sem, 1)

    def dve_scale(self, dve, it):
        dve.wait_ge(self.rstd_ready.sem, self.rstd_ready.at(it, 1))
        rstd = self.rstd[:, :].rearrange("p (a t) -> p a t", a=1).broadcast_to([P, KD, T])
        dve.tensor_tensor(self.xn[:, :, :], self.xc[:, :, :], rstd, ALU.mult).then_inc(self.xn_ready.sem, 1)

    def act_squares(self, act, it):
        act.wait_ge(self.centered_ready.sem, self.centered_ready.at(it, 1))
        act.activation(self.sq[:, :, :], self.xc[:, :, :], ACT.Square).then_inc(self.squares_ready.sem, 1)

    def act_rstd(self, act, it):
        act.wait_ge(self.var_ready.sem, self.var_ready.at(it, 1))
        act.activation(self.rstd[:, :], self.ps[:, 1, :], ACT.Ln, bias=self.K.eps[:, :]).then_inc(self.log_ready.sem, 1)
        act.wait_ge(self.log_ready.sem, self.log_ready.at(it, 1))
        act.activation(self.rstd[:, :], self.rstd[:, :], ACT.Exp, scale=-0.5).then_inc(self.rstd_ready.sem, 1)


def cross_attention(nc, K, name, H, hd, w, scale=1.0, scale_in=None, ffn=None):
    A = H * hd
    NC = A // P
    nh = P // hd
    NP = H // 2
    SW = H * KEYS
    SB = -(-SW // BANK)
    CB = nh * KEYS
    VB = -(-A // BANK)
    OW = 2 * (hd + 1)
    with ExitStack() as ctx:
        s = Section(nc, ctx, name)
        ps = ctx.enter_context(nc.psum_tensor(f"{name}_ps", [P, 8, BANK], F32))
        ln = LayerNorm(s, K, ps)
        wq = s.sb("wq", [P, KD, A])
        wk = s.sb("wk", [P, 2, A])
        wv = s.sb("wv", [P, 2, A])
        HF = 4 if ffn else 0
        wo = s.sb("wo", [P, NC, D]) if not ffn else None
        w1 = s.sb("w1", [P, NC, 2 * D]) if ffn else None
        w2 = s.sb("w2", [P, HF, D]) if ffn else None
        b1 = s.sb("b1", [P, HF]) if ffn else None
        biased = w["bq"] is not None
        bq = s.sb("bq", [P, NC]) if biased else None
        bk = s.sb("bk", [P, NC]) if biased else None
        bv = s.sb("bv", [P, NC]) if biased else None
        bo = s.sb("bo", [P, KD])
        qscale = s.sb("qscale", [P, 1]) if scale_in is not None else None
        ctx_b = s.sb("ctx", [P, 2, P])
        kblk = s.sb("kblk", [P, NC, nh, KEYS])
        vblk = s.sb("vblk", [P, NP, OW])
        negpair = s.sb("negpair", [16, 16, KEYS], BF16)
        qT = s.sb("qT", [P, NC, T])
        mtok = s.sb("max_by_token", [P, NT, H])
        mT = s.sb("max_by_head", [H, T], BF16)
        prob = s.sb("prob", [P, 2, T])
        rec = s.sb("recip", [P, 2, NT, 2])
        otok = s.sb("out_by_token", [P, NT, A])
        oT = s.sb("outT", [P, NC, T])
        hid = s.sb("hid", [P, HF, T]) if ffn else None

        qTu = qT[:, :, :].bitcast(BF16).rearrange("p c (t half) -> p c t half", half=2)[:, :, :, 1]
        kblku = kblk[:, :, :, :].bitcast(BF16).rearrange("p c j (n half) -> p c j n half", half=2)[:, :, :, :, 1]

        kv_loaded, loaded = s.sig("wk_wv_loaded"), s.sig("weights_loaded")
        ctx_ready = s.sig("ctx_ready")
        vclear = s.sig("vblk_cleared")
        k_ready, kblk_ready = s.sig("k_ready"), s.sig("kblk_ready")
        v_ready, vblk_ready = s.sig("v_ready"), s.sig("vblk_ready")
        q_ready, q_taken = s.sig("q_ready", NC), s.sig("q_taken", NC)
        s_ready, s_max = s.sig("scores_ready", NT), s.sig("scores_maxed", NT)
        mt_ready, mt_taken = s.sig("max_turned"), s.sig("max_taken")
        st_ready, p_ready = s.sig("scoresT_ready", NP), s.sig("prob_ready", NP)
        o_ready, o_norm = s.sig("out_ready", NP), s.sig("out_normed", NP)
        ot_ready, ot_taken = s.sig("outT_ready", NC), s.sig("outT_taken", NC)
        h_ready, h_taken = s.sig("hid_ready", 4), s.sig("hid_taken", 4)
        y_ready, x_done = s.sig("y_ready"), s.sig("x_done", ahead=1)
        rec_ready = s.sig("recip_ready", NP)
        block = s.block()

        n_loads = [0]

        @block.sync
        def _(sp):
            def load(dst, src):
                n_loads[0] += 16
                sp.dma_start(dst, src).then_inc(loaded.sem, 16)

            for dst, src in ((wk, w["wk"]), (wv, w["wv"])):
                sp.dma_start(dst[:, 0, :], src[0:P, :]).then_inc(kv_loaded.sem, 16)
                sp.dma_start(dst[0:64, 1, :], src[P:DC, :]).then_inc(kv_loaded.sem, 16)
            load(wq[:, :, :], w["wq"].rearrange("(k p) n -> p k n", p=P))
            if ffn:
                load(w1[:, :, :], w["w1"].rearrange("(k p) n -> p k n", p=P))
                load(w2[:, :, :], w["w2"].rearrange("(k p) n -> p k n", p=P))
                load(b1[:, :], w["b1"])
            else:
                load(wo[:, :, :], w["wo"].rearrange("(k p) n -> p k n", p=P))
            load(bo[:, :], w["bo"])
            if biased:
                load(bq[:, :], w["bq"])
                load(bk[:, :], w["bk"])
                load(bv[:, :], w["bv"])
            if scale_in is not None:
                load(qscale[:, :], scale_in.rearrange("(a n) -> a n", a=1).broadcast_to([P, 1]))
            sp.wait_ge(kv_loaded.sem, 64)
            sp.wait_ge(loaded.sem, n_loads[0])

        def fill_ctx(dve, b, it):
            for half in range(2):
                ins = dve.tensor_scalar(ctx_b[:, :, half * KEYS:(half + 1) * KEYS], K.ctxT[:, :, bass.ds(b, 1), :],
                                        1.0, None, ALU.mult)
            ins.then_inc(ctx_ready.sem, 1)

        @block.tensor
        def _(pe):
            with pe.Fori(0, B) as it:
                pe.wait_ge(x_done.sem, x_done.at(it))
                ln.pe_mean(pe, lambda k: K.x[:, k, bass.ds(it, 1), 1:T + 1])
                pe.wait_ge(ctx_ready.sem, ctx_ready.at(it, 1))
                pe.wait_ge(kv_loaded.sem, 64)
                for c in range(NC):
                    for k, rows in CK:
                        ins = pe.matmul(ps[:, 2, c * KEYS:(c + 1) * KEYS], wk[0:rows, k, c * P:(c + 1) * P],
                                        ctx_b[0:rows, k, 0:KEYS], start=k == 0, stop=k == 1)
                ins.then_inc(k_ready.sem, 1)
                for n in range(VB):
                    width = min(BANK, A)
                    for k, rows in CK:
                        ins = pe.matmul(ps[:, 3 + n, 0:width], ctx_b[0:rows, k, :],
                                        wv[0:rows, k, n * width:(n + 1) * width], start=k == 0, stop=k == 1)
                ins.then_inc(v_ready.sem, 1)
                ln.pe_var(pe, it)
                pe.wait_ge(ln.xn_ready.sem, ln.xn_ready.at(it, 1))
                pe.wait_ge(loaded.sem, n_loads[0])
                for c in range(NC):
                    if c >= 3:
                        pe.wait_ge(q_taken.sem, q_taken.at(it, c - 2))
                    for k in range(KD):
                        ins = pe.matmul(ps[:, 5 + c % 3, :], wq[:, k, c * P:(c + 1) * P], ln.xn[:, k, :],
                                        start=k == 0, stop=k == KD - 1)
                    ins.then_inc(q_ready.sem, 1)
                pe.wait_ge(kblk_ready.sem, kblk_ready.at(it, 1))
                pe.wait_ge(vblk_ready.sem, vblk_ready.at(it, 1))
                pe.wait_ge(q_taken.sem, q_taken.at(it, NC))
                for t in range(NT):
                    base = 2 * (t % 2)
                    if t >= 2:
                        pe.wait_ge(s_max.sem, s_max.at(it, t - 1))
                    for c in range(NC):
                        at = c * CB
                        ins = pe.matmul(ps[:, base + at // BANK, at % BANK:at % BANK + CB], qTu[:, c, t * P:(t + 1) * P],
                                        kblku[:, c, :, :], start=True, stop=True)
                    ins.then_inc(s_ready.sem, 1)
                pe.wait_ge(s_max.sem, s_max.at(it, NT))
                for t in range(NT):
                    ins = pe.transpose(ps[0:H, 4, t * P:(t + 1) * P], mtok[:, t, :], K.ident[:, :])
                ins.then_inc(mt_ready.sem, 1)
                pe.wait_ge(mt_taken.sem, mt_taken.at(it, 1))

                def scoresT(j):
                    if j >= 2:
                        pe.wait_ge(p_ready.sem, p_ready.at(it, j - 1))
                    c, h = 2 * j // nh, 2 * j % nh
                    pe.matmul(ps[:, 5 + j % 2, :], kblk[:, c, h:h + 2, :], qT[:, c, :], start=True, stop=False)
                    pe.matmul(ps[:, 5 + j % 2, :], negpair[0:H, 2 * j:2 * j + 2, :], mT[:, :], start=False, stop=True)\
                        .then_inc(st_ready.sem, 1)

                def values(j):
                    pe.wait_ge(p_ready.sem, p_ready.at(it, j + 1))
                    base = 2 * (j % 2)
                    if j >= 2:
                        pe.wait_ge(o_norm.sem, o_norm.at(it, j - 1))
                    for t in range(NT):
                        ins = pe.matmul(ps[:, base + t // 2, (t % 2) * OW:(t % 2 + 1) * OW],
                                        prob[:, j % 2, t * P:(t + 1) * P], vblk[:, j, :], start=True, stop=True)
                    ins.then_inc(o_ready.sem, 1)

                scoresT(0)
                for j in range(NP):
                    if j + 1 < NP:
                        scoresT(j + 1)
                    values(j)
                pe.wait_ge(o_norm.sem, o_norm.at(it, NP))

                def turn(c):
                    if c >= 2:
                        pe.wait_ge(ot_taken.sem, ot_taken.at(it, c - 1))
                    for t in range(NT):
                        ins = pe.transpose(ps[:, 4 + 3 * (c % 2), t * P:(t + 1) * P], otok[:, t, c * P:(c + 1) * P],
                                           K.ident[:, :])
                    ins.then_inc(ot_ready.sem, 1)

                turn(0)
                for c in range(NC):
                    if c + 1 < NC:
                        turn(c + 1)
                    pe.wait_ge(ot_taken.sem, ot_taken.at(it, c + 1))
                    if not ffn:
                        for m in range(KD):
                            ins = pe.matmul(ps[:, 5 + m, :], wo[:, c, m * P:(m + 1) * P], oT[:, c, :],
                                            start=c == 0, stop=c == NC - 1)
                if ffn:
                    for f in range(HF):
                        for c in range(NC):
                            ins = pe.matmul(ps[:, f, :], w1[:, c, f * P:(f + 1) * P], oT[:, c, :],
                                            start=c == 0, stop=c == NC - 1)
                        ins.then_inc(h_ready.sem, 1)
                    for f in range(HF):
                        pe.wait_ge(h_taken.sem, h_taken.at(it, f + 1))
                        for m in range(KD):
                            ins = pe.matmul(ps[:, 5 + m, :], w2[:, f, m * P:(m + 1) * P], hid[:, f, :],
                                            start=f == 0, stop=f == HF - 1)
                ins.then_inc(y_ready.sem, 1)

        @block.vector
        def _(dve):
            x_done.raise_ahead(dve)
            dve.memset(vblk[:, :, :], 0.0).then_inc(vclear.sem, 1)
            dve.wait_ge(vclear.sem, 1)
            dve.tensor_copy(negpair[:, :, :], K.negident[:, :].rearrange("h (j e) -> h j e", e=1).broadcast_to([16, 16, KEYS]))
            dve.memset(vblk[0:KEYS, :, hd:hd + 1], 1.0)
            dve.memset(vblk[KEYS:P, :, OW - 1:OW], 1.0).then_inc(vclear.sem, 1)
            with dve.Fori(0, B) as it:
                dve.wait_ge(x_done.sem, x_done.at(it))
                fill_ctx(dve, it, it)
                ln.dve_center(dve, it, K.x[:, :, bass.ds(it, 1), 1:T + 1])
                dve.wait_ge(k_ready.sem, k_ready.at(it, 1))
                dve.wait_ge(loaded.sem, n_loads[0])
                if not biased:
                    for j in range(nh):
                        ins = dve.tensor_scalar(kblk[:, :, j, :], ps[:, 2, 0:NC * KEYS].rearrange("p (c n) -> p c n", c=NC),
                                                K.rows(hd, j), None, ALU.mult)
                else:
                    for c in range(NC):
                        for j in range(nh):
                            ins = dve.tensor_scalar(kblk[:, c, j, :], ps[:, 2, c * KEYS:(c + 1) * KEYS],
                                                    bk[:, c:c + 1], K.rows(hd, j), ALU.add, ALU.mult)
                ins.then_inc(kblk_ready.sem, 1)
                ln.dve_scale(dve, it)
                if biased:
                    for c in range(NC):
                        dve.wait_ge(q_ready.sem, q_ready.at(it, c + 1))
                        if scale_in is not None:
                            dve.tensor_scalar(qT[:, c, :], ps[:, 5 + c % 3, :], bq[:, c:c + 1], qscale[:, 0:1],
                                              ALU.add, ALU.mult).then_inc(q_taken.sem, 1)
                        else:
                            dve.tensor_scalar(qT[:, c, :], ps[:, 5 + c % 3, :], bq[:, c:c + 1], None,
                                              ALU.add).then_inc(q_taken.sem, 1)
                for t in range(NT):
                    dve.wait_ge(s_ready.sem, s_ready.at(it, t + 1))
                    base = 2 * (t % 2)
                    banks = ps[:, base:base + SB, 0:min(SW, BANK)].rearrange("p a (h n) -> p (a h) n", n=KEYS)
                    dve.tensor_reduce(mtok[:, t, :], banks, AX.X, ALU.max).then_inc(s_max.sem, 1)
                dve.wait_ge(mt_ready.sem, mt_ready.at(it, 1))
                dve.tensor_copy(mT[:, :], ps[0:H, 4, :]).then_inc(mt_taken.sem, 1)
                for j in range(NP):
                    dve.wait_ge(o_ready.sem, o_ready.at(it, j + 1))
                    base = 2 * (j % 2)
                    out = ps[:, base:base + 2, 0:2 * OW].rearrange("p a (t g e) -> p a t g e", t=2, g=2)
                    for a in range(2):
                        ins = dve.reciprocal(rec[:, j % 2, 2 * a:2 * a + 2, :], out[:, a, :, :, hd])
                    ins.then_inc(rec_ready.sem, 1)
                    dve.wait_ge(rec_ready.sem, rec_ready.at(it, j + 1))
                    for a in range(2):
                        r = rec[:, j % 2, 2 * a:2 * a + 2, :].rearrange("p t (g e) -> p t g e", e=1)
                        ins = dve.tensor_tensor(
                            otok[:, 2 * a:2 * a + 2, 2 * j * hd:2 * (j + 1) * hd].rearrange("p t (g e) -> p t g e", g=2),
                            out[:, a, :, :, 0:hd], r.broadcast_to([P, 2, 2, hd]), ALU.mult)
                    ins.then_inc(o_norm.sem, 1)
                dve.wait_ge(y_ready.sem, y_ready.at(it, 1))
                for m in range(KD):
                    xm = K.x[:, m, bass.ds(it, 1), 1:T + 1].rearrange("p a t -> p (a t)")
                    ins = dve.scalar_tensor_tensor(out=xm, in0=ps[:, 5 + m, :], scalar=bo[:, m:m + 1], in1=xm,
                                                   op0=ALU.add, op1=ALU.add)
                ins.then_inc(x_done.sem, 1)

        @block.scalar
        def _(act):
            act.preload_act_table_set("natural_log_exp_and_others")
            act.wait_ge(vclear.sem, 2)
            with act.Fori(0, B) as it:
                ln.act_squares(act, it)
                act.wait_ge(v_ready.sem, v_ready.at(it, 1))
                for g in range(2):
                    half = slice(g * KEYS, (g + 1) * KEYS)
                    width = min(BANK, A)
                    src = ps[half, 3:3 + VB, 0:width].rearrange("p a (j g e) -> p (a j) g e", g=2, e=hd)
                    ins = act.activation(vblk[half, :, g * (hd + 1):g * (hd + 1) + hd], src[:, :, g, :], ACT.Copy)
                ins.then_inc(vblk_ready.sem, 1)
                ln.act_rstd(act, it)
                if not biased:
                    for c in range(NC):
                        act.wait_ge(q_ready.sem, q_ready.at(it, c + 1))
                        act.activation(qT[:, c, :], ps[:, 5 + c % 3, :], ACT.Copy).then_inc(q_taken.sem, 1)
                for j in range(NP):
                    act.wait_ge(st_ready.sem, st_ready.at(it, j + 1))
                    if j >= 2:
                        act.wait_ge(o_ready.sem, o_ready.at(it, j - 1))
                    act.activation(prob[:, j % 2, :], ps[:, 5 + j % 2, :], ACT.Exp, scale=scale).then_inc(p_ready.sem, 1)
                for c in range(NC):
                    act.wait_ge(ot_ready.sem, ot_ready.at(it, c + 1))
                    if biased:
                        act.activation(oT[:, c, :], ps[:, 4 + 3 * (c % 2), :], ACT.Identity, bias=bv[:, c:c + 1])\
                            .then_inc(ot_taken.sem, 1)
                    else:
                        act.activation(oT[:, c, :], ps[:, 4 + 3 * (c % 2), :], ACT.Copy).then_inc(ot_taken.sem, 1)
                for f in range(HF):
                    act.wait_ge(h_ready.sem, h_ready.at(it, f + 1))
                    act.activation(hid[:, f, :], ps[:, f, :], ACT.Relu, bias=b1[:, f:f + 1]).then_inc(h_taken.sem, 1)


def enter_inner_stream(nc, K, saved):
    with ExitStack() as ctx:
        s = Section(nc, ctx, "enter")
        ps = ctx.enter_context(nc.psum_tensor("enter_ps", [P, 8, BANK], F32))
        ln = LayerNorm(s, K, ps)
        x_saved, x_done = s.sig("x_saved"), s.sig("x_done", ahead=1)
        block = s.block()

        @block.sync
        def _(sp):
            for k in range(KD):
                sp.dma_start(saved[k * P:(k + 1) * P, :].rearrange("p (b t) -> p b t", b=B), K.x[:, k, :, 1:T + 1])\
                    .then_inc(x_saved.sem, 16)
            sp.wait_ge(x_saved.sem, 16 * KD)

        @block.tensor
        def _(pe):
            with pe.Fori(0, B) as it:
                pe.wait_ge(x_done.sem, x_done.at(it))
                ln.pe_mean(pe, lambda k: K.x[:, k, bass.ds(it, 1), 1:T + 1])
                ln.pe_var(pe, it)

        @block.scalar
        def _(act):
            act.preload_act_table_set("natural_log_exp_and_others")
            with act.Fori(0, B) as it:
                ln.act_squares(act, it)
                ln.act_rstd(act, it)

        @block.vector
        def _(dve):
            x_done.raise_ahead(dve)
            dve.wait_ge(x_saved.sem, 16 * KD)
            with dve.Fori(0, B) as it:
                ln.dve_center(dve, it, K.x[:, :, bass.ds(it, 1), 1:T + 1])
                dve.wait_ge(ln.rstd_ready.sem, ln.rstd_ready.at(it, 1))
                for k in range(KD):
                    xk = K.x[:, k, bass.ds(it, 1), 1:T + 1].rearrange("p a t -> p (a t)")
                    ins = dve.tensor_tensor(xk, ln.xc[:, k, :], ln.rstd[:, :], ALU.mult)
                ins.then_inc(x_done.sem, 1)


def leave_inner_stream(nc, K, saved):
    with ExitStack() as ctx:
        s = Section(nc, ctx, "leave")
        before = s.sb("x_before", [P, KD, B, T])
        loaded = s.sig("x_loaded")
        block = s.block()

        @block.sync
        def _(sp):
            for k in range(KD):
                sp.dma_start(before[:, k, :, :], saved[k * P:(k + 1) * P, :].rearrange("p (b t) -> p b t", b=B))\
                    .then_inc(loaded.sem, 16)

        @block.vector
        def _(dve):
            dve.wait_ge(loaded.sem, 16 * KD)
            for k in range(KD):
                x = K.x[:, k, :, 1:T + 1]
                dve.tensor_tensor(x, x, before[:, k, :, :], ALU.add)


def bitnet(nc, K, a):
    HID = 1024
    NH = HID // P
    MAGIC = 1.5 * 2 ** 23
    with ExitStack() as ctx:
        s = Section(nc, ctx, "l1f")
        ps = ctx.enter_context(nc.psum_tensor("l1f_ps", [P, 8, BANK], F32))
        ln = LayerNorm(s, K, ps)
        w = s.sb("weights", [P, 2, 2 * HID])
        wq = s.sb("weights_rounded", [P, 2, 2 * HID], BF16)
        wsum = s.sb("weight_sums", [P, 2])
        wmean = s.sb("weight_mean", [P, 2])
        winv = s.sb("weight_scale", [P, 2])
        identb = K.identb
        ones = s.sb("ones", [P, P])
        cw = s.sb("conv_w", [P, NH, 3])
        cb = s.sb("conv_b", [P, NH])
        amax = s.sb("act_max", [P, NT])
        asc = s.sb("act_scale", [P, NT])
        ainv = s.sb("act_step", [P, NT])
        tmp = s.sb("rounding", [P, HID])
        xqt = s.sb("x_rounded", [P, 2, HID], BF16)
        dg = s.sb("step_diagonal", [P, NT, P])
        step_b = s.sb("act_step_spread", [P, T])
        xq = s.sb("x_roundedT", [P, NH, T], BF16)
        hp = s.sb("hidden_padded", [P, 2, T + 2])
        cv = s.sb("conv", [P, 2, T])
        hs = s.sb("hidden", [P, NH, T])
        loaded = s.sig("loaded", 16 * 4)
        ws_ready, wm_ready = s.sig("weight_sums_ready"), s.sig("weight_means_ready")
        w_ready = s.sig("weights_ready", 2)
        xt_ready, xq_ready, qt_ready, xq_taken = s.sig("by_token_ready", 8), s.sig("rounded_ready", 8), s.sig("roundedT_ready", 5), s.sig("roundedT_taken", 5)
        dg_ready, sb_ready, sb_taken = s.sig("diagonal_ready", 2), s.sig("step_ready", 2), s.sig("step_taken", 2)
        h_ready, h_taken, conv_ready, hs_ready = s.sig("up_ready", NH), s.sig("up_taken", NH), s.sig("conv_ready", NH), s.sig("hidden_ready", NH)
        y_ready, x_done = s.sig("y_ready"), s.sig("x_done", ahead=1)
        setup_step = s.sig("setup_step", 6)
        dve_step = s.sig("dve_step", 5 + 2 * NT + 2 * NH + 6 * NT + 2)
        block = s.block()

        @block.sync
        def _(sp):
            for dst, src in ((w[:, 0, :].rearrange("p (k n) -> p k n", k=KD), a["L1_ffn_w1"].rearrange("(k p) n -> p k n", p=P)),
                             (w[:, 1, :].rearrange("p (k n) -> p k n", k=NH), a["L1_ffn_w2"].rearrange("(k p) n -> p k n", p=P)),
                             (cw[:, :, :], a["conv_w_columns"].rearrange("p (k n) -> p k n", k=NH)),
                             (cb[:, :], a["L1_ffn_conv_b"])):
                sp.dma_start(dst, src).then_inc(loaded.sem, 16)
            sp.wait_ge(loaded.sem, loaded.per)

        flat = xqt[:, :, :].rearrange("p u n -> p (u n)")
        w1q = wq[:, 0, :].rearrange("p (k n) -> p k n", k=KD)
        w2q = wq[:, 1, :].rearrange("p (k n) -> p k n", k=NH)

        @block.tensor
        def _(pe):
            pe.wait_ge(ws_ready.sem, 1)
            pe.matmul(ps[:, 0, 0:2], K.mean[:, :], wsum[:, :], start=True, stop=True).then_inc(wm_ready.sem, 1)
            pe.wait_ge(w_ready.sem, 2)
            with pe.Fori(0, B) as it:
                pe.wait_ge(x_done.sem, x_done.at(it))
                ln.pe_mean(pe, lambda k: K.x[:, k, bass.ds(it, 1), 1:T + 1])
                ln.pe_var(pe, it)
                pe.wait_ge(ln.xn_ready.sem, ln.xn_ready.at(it, 1))
                for t in range(NT):
                    for k in range(KD):
                        ins = pe.transpose(ps[:, 2 + t // 2, (t % 2) * D + k * P:(t % 2) * D + (k + 1) * P],
                                           ln.xn[:, k, t * P:(t + 1) * P], K.ident[:, :])
                    ins.then_inc(xt_ready.sem, 1)
                for t in range(NT):
                    pe.wait_ge(xq_ready.sem, xq_ready.at(it, t + 1))
                    for k in range(KD):
                        ins = pe.matmul(ps[:, 4 + k, t * P:(t + 1) * P], flat[:, t * D + k * P:t * D + (k + 1) * P], identb[:, :],
                                        start=True, stop=True)
                ins.then_inc(qt_ready.sem, 1)

                def spread(n):
                    pe.wait_ge(dg_ready.sem, dg_ready.at(it, n + 1))
                    for t in range(NT):
                        ins = pe.matmul(ps[:, 6, t * P:(t + 1) * P], ones[:, :], dg[:, t, :], start=True, stop=True)
                    ins.then_inc(sb_ready.sem, 1)

                spread(0)
                pe.wait_ge(xq_taken.sem, xq_taken.at(it, 1))
                for c in range(NH):
                    if c >= 2:
                        pe.wait_ge(h_taken.sem, h_taken.at(it, c - 1))
                    for k in range(KD):
                        ins = pe.matmul(ps[:, 2 + c % 2, :], w1q[:, k, c * P:(c + 1) * P], xq[:, k, :],
                                        start=k == 0, stop=k == KD - 1)
                    ins.then_inc(h_ready.sem, 1)
                pe.wait_ge(hs_ready.sem, hs_ready.at(it, NH))

                def turn(t):
                    base = 2 * (t % 2)
                    if t >= 2:
                        pe.wait_ge(xq_ready.sem, xq_ready.at(it, 4 + t - 1))
                    for c in range(NH):
                        ins = pe.transpose(ps[:, base + c // 4, (c % 4) * P:(c % 4 + 1) * P], hs[:, c, t * P:(t + 1) * P],
                                           K.ident[:, :])
                    ins.then_inc(xt_ready.sem, 1)

                def turn_back(t):
                    pe.wait_ge(xq_ready.sem, xq_ready.at(it, 4 + t + 1))
                    pe.wait_ge(xq_taken.sem, xq_taken.at(it, 1 + t))
                    for c in range(NH):
                        ins = pe.matmul(ps[:, 4 + c // 4, (c % 4) * P:(c % 4 + 1) * P], xqt[:, t % 2, c * P:(c + 1) * P],
                                        identb[:, :], start=True, stop=True)
                    ins.then_inc(qt_ready.sem, 1)

                pe.wait_ge(h_taken.sem, h_taken.at(it, NH))
                turn(0)
                for t in range(NT):
                    if t + 1 < NT:
                        turn(t + 1)
                    turn_back(t)
                spread(1)
                pe.wait_ge(xq_taken.sem, xq_taken.at(it, 5))
                for m in range(KD):
                    for c in range(NH):
                        ins = pe.matmul(ps[:, m, :], w2q[:, c, m * P:(m + 1) * P], xq[:, c, :], start=c == 0, stop=c == NH - 1)
                ins.then_inc(y_ready.sem, 1)

        @block.vector
        def _(dve):
            x_done.raise_ahead(dve)
            dve.memset(ones[:, :], 1.0)
            dve.memset(hp[:, :, :], 0.0)
            dve.wait_ge(loaded.sem, loaded.per)
            step = Chain(dve, setup_step, 0)
            for n in range(2):
                ins = dve.tensor_reduce(wsum[:, n:n + 1], w[:, n, :], AX.X, ALU.add, apply_absolute_value=True)
            ins.then_inc(ws_ready.sem, 1)
            dve.wait_ge(wm_ready.sem, 1)
            step(dve.tensor_scalar(wmean[:, :], ps[:, 0, 0:2], 1.0 / HID, 1e-5, ALU.mult, ALU.max))
            step(dve.reciprocal(winv[:, :], wmean[:, :]))
            for n in range(2):
                step(dve.tensor_scalar(w[:, n, :], w[:, n, :], winv[:, n:n + 1], 1.0, ALU.mult, ALU.min))
                step(dve.tensor_scalar(w[:, n, :], w[:, n, :], -1.0, MAGIC, ALU.max, ALU.add))
                dve.tensor_scalar(wq[:, n, :], w[:, n, :], MAGIC, None, ALU.subtract).then_inc(w_ready.sem, 1)
            step.end()
            with dve.Fori(0, B) as it:
                dve.wait_ge(x_done.sem, x_done.at(it))
                step = Chain(dve, dve_step, it)
                ln.dve_center(dve, it, K.x[:, :, bass.ds(it, 1), 1:T + 1])
                ln.dve_scale(dve, it)

                def scales(cols, src):
                    step(dve.tensor_reduce(amax[:, cols], src, AX.X, ALU.max, apply_absolute_value=True))
                    step(dve.tensor_scalar(amax[:, cols], amax[:, cols], 1e-5, None, ALU.max))
                    step(dve.reciprocal(asc[:, cols], amax[:, cols]))
                    step(dve.tensor_scalar(asc[:, cols], asc[:, cols], 127.0, None, ALU.mult))

                def rounded(dst, src, width, t, n):
                    step(dve.tensor_scalar(tmp[:, 0:width], src, asc[:, t:t + 1], 127.0, ALU.mult, ALU.min))
                    step(dve.tensor_scalar(tmp[:, 0:width], tmp[:, 0:width], -128.0, MAGIC, ALU.max, ALU.add))
                    dve.tensor_scalar(dst, tmp[:, 0:width], MAGIC, None, ALU.subtract).then_inc(xq_ready.sem, 1)
                    dve.wait_ge(xq_ready.sem, xq_ready.at(it, n))

                def diagonals():
                    step(dve.tensor_scalar(ainv[:, :], amax[:, :], 1.0 / 127.0, None, ALU.mult))
                    for t in range(NT):
                        ins = dve.tensor_scalar(dg[:, t, :], K.ident[:, :], ainv[:, t:t + 1], None, ALU.mult)
                    ins.then_inc(dg_ready.sem, 1)

                dve.wait_ge(xt_ready.sem, xt_ready.at(it, NT))
                scales(slice(0, NT), ps[:, 2:4, :].rearrange("p a (t n) -> p (a t) n", n=D))
                for t in range(NT):
                    rounded(flat[:, t * D:(t + 1) * D], ps[:, 2 + t // 2, (t % 2) * D:(t % 2 + 1) * D], D, t, t + 1)
                diagonals()
                dve.wait_ge(sb_taken.sem, sb_taken.at(it, 1))
                for c in range(NH):
                    dve.wait_ge(h_ready.sem, h_ready.at(it, c + 1))
                    dve.tensor_tensor(hp[:, c % 2, 1:T + 1], ps[:, 2 + c % 2, :], step_b[:, :], ALU.mult)\
                        .then_inc(h_taken.sem, 1)
                    dve.wait_ge(h_taken.sem, h_taken.at(it, c + 1))
                    if c >= 2:
                        dve.wait_ge(hs_ready.sem, hs_ready.at(it, c - 1))
                    step(dve.tensor_scalar(cv[:, c % 2, :], hp[:, c % 2, 0:T], cw[:, c, 0:1], None, ALU.mult))
                    step(dve.scalar_tensor_tensor(out=cv[:, c % 2, :], in0=hp[:, c % 2, 1:T + 1], scalar=cw[:, c, 1:2],
                                                  in1=cv[:, c % 2, :], op0=ALU.mult, op1=ALU.add))
                    dve.scalar_tensor_tensor(out=cv[:, c % 2, :], in0=hp[:, c % 2, 2:T + 2], scalar=cw[:, c, 2:3],
                                             in1=cv[:, c % 2, :], op0=ALU.mult, op1=ALU.add).then_inc(conv_ready.sem, 1)
                for t in range(NT):
                    base = 2 * (t % 2)
                    src = ps[:, base:base + 2, :].rearrange("p a n -> p (a n)")
                    dve.wait_ge(xt_ready.sem, xt_ready.at(it, NT + t + 1))
                    scales(slice(t, t + 1), src)
                    dve.wait_ge(qt_ready.sem, qt_ready.at(it, max(1, t)))
                    rounded(xqt[:, t % 2, :], src, HID, t, t + 1)
                diagonals()
                dve.wait_ge(sb_taken.sem, sb_taken.at(it, 2))
                dve.wait_ge(y_ready.sem, y_ready.at(it, 1))
                for m in range(KD):
                    ins = dve.tensor_tensor(cv[:, m, :], ps[:, m, :], step_b[:, :], ALU.mult)
                step(ins)
                step.end()
                xb = K.x[:, :, bass.ds(it, 1), 1:T + 1].rearrange("p k a t -> p (k a) t")
                dve.tensor_tensor(xb, xb, cv[:, :, :], ALU.add).then_inc(x_done.sem, 1)

        @block.scalar
        def _(act):
            act.wait_ge(loaded.sem, loaded.per)
            act.wait_ge(wm_ready.sem, 1)
            with act.Fori(0, B) as it:
                act.preload_act_table_set("natural_log_exp_and_others")
                ln.act_squares(act, it)
                ln.act_rstd(act, it)

                def spread(n):
                    act.wait_ge(sb_ready.sem, sb_ready.at(it, n + 1))
                    act.activation(step_b[:, :], ps[:, 6, :], ACT.Copy, scale=wmean[:, n:n + 1]).then_inc(sb_taken.sem, 1)

                act.wait_ge(qt_ready.sem, qt_ready.at(it, 1))
                act.activation(xq[:, 0:KD, :], ps[:, 4:6, :], ACT.Copy).then_inc(xq_taken.sem, 1)
                spread(0)
                for c in range(NH):
                    act.wait_ge(conv_ready.sem, conv_ready.at(it, c + 1))
                    act.activation(hs[:, c, :], cv[:, c % 2, :], ACT.Silu, bias=cb[:, c:c + 1]).then_inc(hs_ready.sem, 1)
                for t in range(NT):
                    act.wait_ge(qt_ready.sem, qt_ready.at(it, t + 2))
                    act.activation(xq[:, :, t * P:(t + 1) * P], ps[:, 4:6, :].rearrange("p a (c n) -> p (a c) n", n=P),
                                   ACT.Copy).then_inc(xq_taken.sem, 1)
                act.wait_ge(h_taken.sem, h_taken.at(it, NH))
                spread(1)


def experts(nc, K, a):
    E, HID = 8, 128
    N = E + 1
    with ExitStack() as ctx:
        s = Section(nc, ctx, "l3f")
        ps = ctx.enter_context(nc.psum_tensor("l3f_ps", [P, 8, BANK], F32))
        ln = LayerNorm(s, K, ps)
        w1 = s.sb("w1", [P, N, KD, HID])
        w2 = s.sb("w2", [P, N, D])
        b1 = s.sb("b1", [P, N])
        rb2 = s.sb("rb2", [E, D])
        sb2 = s.sb("sb2", [P, KD])
        rw = s.sb("routing", [P, KD, E])
        rbias = s.sb("routing_bias", [P, E])
        before = s.sb("index_before", [P, E * E])
        pick = s.sb("pick", [E, E, P])
        lg = s.sb("logits", [P, NT, E])
        ex = s.sb("exp_neg_abs", [P, NT, E])
        u = s.sb("one_plus", [P, NT, E])
        lu = s.sb("log_one_plus", [P, NT, E])
        tmp = s.sb("tmp", [P, NT, E])
        sp_ = s.sb("activation", [P, NT, E])
        gt = s.sb("greater", [P, NT, E * E])
        eq = s.sb("equal", [P, NT, E * E])
        cf = s.sb("weights", [P, NT, E])
        cfT = s.sb("weightsT", [E, T])
        hs = s.sb("hidden", [P, 2, T])
        hc = s.sb("hidden_weighted", [P, 2, T])
        loaded = s.sig("loaded", 16 * 12)
        lg_ready, na_ready, explog_ready = s.sig("logits_ready"), s.sig("neg_abs_ready"), s.sig("exp_and_log_ready", 2)
        sp_ready, act_ready = s.sig("softplus_ready"), s.sig("activation_ready")
        cf_ready, ct_ready, cfT_ready = s.sig("weights_ready"), s.sig("weights_turned"), s.sig("weightsT_ready")
        u_ready, h_ready, hs_ready, hc_ready = s.sig("up_ready", N), s.sig("spread_ready", E), s.sig("hidden_ready", N), s.sig("weighted_ready", E)
        y_ready, x_done = s.sig("y_ready"), s.sig("x_done", ahead=1)
        down_done = s.sig("down_done", N)
        dve_step = s.sig("dve_step", 12)
        block = s.block()

        @block.sync
        def _(sp):
            for dst, src in ((rw[:, :, :], a["L3_ffn_routing_W"].rearrange("(k p) n -> p k n", p=P)),
                             (rbias[:, :], a["L3_ffn_expert_bias"].rearrange("(o n) -> o n", o=1).broadcast_to([P, E])),
                             (before[:, :], a["index_before"].rearrange("(o n) -> o n", o=1).broadcast_to([P, E * E])),
                             (pick[:, :, :], a["pick"].rearrange("h (j n) -> h j n", j=E)),
                             (w1[:, 0:E, :, :], a["L3_ffn_rW1"].rearrange("e (k p) n -> p e k n", p=P)),
                             (w1[:, E, :, :], a["L3_ffn_sW1"].rearrange("(k p) n -> p k n", p=P)),
                             (w2[:, 0:E, :], a["L3_ffn_rW2"].rearrange("e p n -> p e n")),
                             (w2[:, E, :], a["L3_ffn_sW2"]),
                             (b1[:, 0:E], a["L3_ffn_rb1"]), (b1[:, E:N], a["L3_ffn_sb1"]),
                             (rb2[:, :], a["L3_ffn_rb2"]), (sb2[:, :], a["L3_ffn_sb2"])):
                sp.dma_start(dst, src).then_inc(loaded.sem, 16)
            sp.wait_ge(loaded.sem, loaded.per)

        @block.tensor
        def _(pe):
            with pe.Fori(0, B) as it:
                pe.wait_ge(x_done.sem, x_done.at(it))
                ln.pe_mean(pe, lambda k: K.x[:, k, bass.ds(it, 1), 1:T + 1])
                ln.pe_var(pe, it)
                pe.wait_ge(ln.xn_ready.sem, ln.xn_ready.at(it, 1))
                pe.wait_ge(loaded.sem, loaded.per)
                for t in range(NT):
                    for k in range(KD):
                        ins = pe.matmul(ps[:, 2, t * E:(t + 1) * E], ln.xn[:, k, t * P:(t + 1) * P], rw[:, k, :],
                                        start=k == 0, stop=k == KD - 1)
                ins.then_inc(lg_ready.sem, 1)

                def up(n):
                    e = (n + E) % N
                    if n >= 2:
                        pe.wait_ge(hs_ready.sem, hs_ready.at(it, n - 1))
                    for k in range(KD):
                        ins = pe.matmul(ps[:, 4 + n % 2, :], w1[:, e, k, :], ln.xn[:, k, :], start=k == 0, stop=k == KD - 1)
                    ins.then_inc(u_ready.sem, 1)
                    if n >= 1:
                        if n >= 3:
                            pe.wait_ge(hc_ready.sem, hc_ready.at(it, n - 2))
                        pe.matmul(ps[:, 6 + n % 2, :], pick[:, e, :], cfT[:, :], start=True, stop=True)\
                            .then_inc(h_ready.sem, 1)

                def down(n):
                    e = (n + E) % N
                    if n == 0:
                        pe.wait_ge(hs_ready.sem, hs_ready.at(it, 1))
                        src = hs[:, 0, :]
                    else:
                        pe.wait_ge(hc_ready.sem, hc_ready.at(it, n))
                        src = hc[:, n % 2, :]
                    for m in range(KD):
                        ins = pe.matmul(ps[:, m, :], w2[:, e, m * P:(m + 1) * P], src, start=n == 0, stop=False)
                    ins.then_inc(down_done.sem, 1)

                up(0)
                down(0)
                pe.wait_ge(cf_ready.sem, cf_ready.at(it, 1))
                for t in range(NT):
                    ins = pe.transpose(ps[0:E, 3, t * P:(t + 1) * P], cf[:, t, :], K.ident[:, :])
                ins.then_inc(ct_ready.sem, 1)
                pe.wait_ge(cfT_ready.sem, cfT_ready.at(it, 1))
                up(1)
                for n in range(1, N):
                    if n + 1 < N:
                        up(n + 1)
                    down(n)
                for m in range(KD):
                    ins = pe.matmul(ps[:, m, :], rb2[:, m * P:(m + 1) * P], cfT[:, :], start=False, stop=True)
                ins.then_inc(y_ready.sem, 1)

        @block.vector
        def _(dve):
            x_done.raise_ahead(dve)
            with dve.Fori(0, B) as it:
                dve.wait_ge(x_done.sem, x_done.at(it))
                step = Chain(dve, dve_step, it)
                ln.dve_center(dve, it, K.x[:, :, bass.ds(it, 1), 1:T + 1])
                ln.dve_scale(dve, it)
                dve.wait_ge(loaded.sem, loaded.per)
                bias = rbias[:, :].rearrange("p (o e) -> p o e", o=1).broadcast_to([P, NT, E])
                dve.wait_ge(lg_ready.sem, lg_ready.at(it, 1))
                step(dve.tensor_tensor(lg[:, :, :], ps[:, 2, 0:NT * E].rearrange("p (t e) -> p t e", e=E), bias, ALU.add))
                dve.scalar_tensor_tensor(out=ex[:, :, :], in0=lg[:, :, :], scalar=-1.0, in1=lg[:, :, :],
                                         op0=ALU.mult, op1=ALU.min).then_inc(na_ready.sem, 1)
                dve.wait_ge(explog_ready.sem, explog_ready.at(it, 1))
                step(dve.tensor_scalar(u[:, :, :], ex[:, :, :], 1.0, None, ALU.add))
                step(dve.tensor_scalar(tmp[:, :, :], u[:, :, :], -1.0, None, ALU.add))
                step(dve.tensor_tensor(tmp[:, :, :], ex[:, :, :], tmp[:, :, :], ALU.subtract))
                dve.wait_ge(explog_ready.sem, explog_ready.at(it, 2))
                step(dve.reciprocal(ex[:, :, :], u[:, :, :]))
                step(dve.tensor_tensor(tmp[:, :, :], tmp[:, :, :], ex[:, :, :], ALU.mult))
                step(dve.tensor_tensor(tmp[:, :, :], tmp[:, :, :], lu[:, :, :], ALU.add))
                dve.scalar_tensor_tensor(out=sp_[:, :, :], in0=lg[:, :, :], scalar=0.0, in1=tmp[:, :, :],
                                         op0=ALU.max, op1=ALU.add).then_inc(sp_ready.sem, 1)
                dve.wait_ge(act_ready.sem, act_ready.at(it, 1))
                for t in range(NT):
                    row = sp_[:, t, :].rearrange("p (o j) -> p o j", o=1).broadcast_to([P, E, E])
                    col = sp_[:, t, :].rearrange("p (e o) -> p e o", o=1).broadcast_to([P, E, E])
                    dve.tensor_tensor(gt[:, t, :].rearrange("p (e j) -> p e j", j=E), row, col, ALU.is_gt)
                    ins = dve.tensor_tensor(eq[:, t, :].rearrange("p (e j) -> p e j", j=E), row, col, ALU.is_equal)
                step(ins)
                tri = before[:, :].rearrange("p (o n) -> p o n", o=1).broadcast_to([P, NT, E * E])
                step(dve.tensor_tensor(eq[:, :, :], eq[:, :, :], tri, ALU.mult))
                step(dve.tensor_tensor(gt[:, :, :], gt[:, :, :], eq[:, :, :], ALU.add))
                step(dve.tensor_reduce(tmp[:, :, :], gt[:, :, :].rearrange("p t (e j) -> p (t e) j", j=E), AX.X, ALU.add))
                step(dve.tensor_scalar(tmp[:, :, :], tmp[:, :, :], 1.5, None, ALU.is_lt))
                dve.tensor_tensor(cf[:, :, :], sp_[:, :, :], tmp[:, :, :], ALU.mult).then_inc(cf_ready.sem, 1)
                step.end()
                for n in range(1, N):
                    dve.wait_ge(hs_ready.sem, hs_ready.at(it, n + 1))
                    dve.wait_ge(h_ready.sem, h_ready.at(it, n))
                    if n >= 3:
                        dve.wait_ge(down_done.sem, down_done.at(it, n - 1))
                    dve.tensor_tensor(hc[:, n % 2, :], hs[:, n % 2, :], ps[:, 6 + n % 2, :], ALU.mult).then_inc(hc_ready.sem, 1)
                dve.wait_ge(y_ready.sem, y_ready.at(it, 1))
                for m in range(KD):
                    xm = K.x[:, m, bass.ds(it, 1), 1:T + 1].rearrange("p a t -> p (a t)")
                    ins = dve.scalar_tensor_tensor(out=xm, in0=ps[:, m, :], scalar=sb2[:, m:m + 1], in1=xm,
                                                   op0=ALU.add, op1=ALU.add)
                ins.then_inc(x_done.sem, 1)

        @block.scalar
        def _(act):
            with act.Fori(0, B) as it:
                act.preload_act_table_set("natural_log_exp_and_others")
                ln.act_squares(act, it)
                ln.act_rstd(act, it)
                act.wait_ge(loaded.sem, loaded.per)
                act.wait_ge(na_ready.sem, na_ready.at(it, 1))
                act.activation(ex[:, :, :], ex[:, :, :], ACT.Exp).then_inc(explog_ready.sem, 1)
                act.wait_ge(explog_ready.sem, explog_ready.at(it, 1))
                act.activation(lu[:, :, :], ex[:, :, :], ACT.Ln, bias=K.one[:, :]).then_inc(explog_ready.sem, 1)
                act.wait_ge(sp_ready.sem, sp_ready.at(it, 1))
                act.activation(sp_[:, :, :], sp_[:, :, :], ACT.Sqrt).then_inc(act_ready.sem, 1)
                for n in range(N):
                    e = (n + E) % N
                    if n == 1:
                        act.wait_ge(ct_ready.sem, ct_ready.at(it, 1))
                        act.activation(cfT[:, :], ps[0:E, 3, :], ACT.Copy).then_inc(cfT_ready.sem, 1)
                    act.wait_ge(u_ready.sem, u_ready.at(it, n + 1))
                    if n == 2:
                        act.wait_ge(down_done.sem, down_done.at(it, 1))
                    if n >= 3:
                        act.wait_ge(hc_ready.sem, hc_ready.at(it, n - 2))
                    act.activation(hs[:, n % 2, :], ps[:, 4 + n % 2, :], ACT.Silu, bias=b1[:, e:e + 1]).then_inc(hs_ready.sem, 1)


def local_transformer(nc, K, a):
    DEPTH, H, hd, W = 6, 16, 64, 64
    INNER = H * hd
    NP = H // 2
    HALF = hd // 2
    F = 682
    NF = -(-F // P)
    FR = F - (NF - 1) * P
    SK = P + W
    QK_SCALE = 8.0
    PASSES = DEPTH * B
    FFN_FROM = 4
    UNITS = (0, 1, 4, 2, 3, 5)
    RING = (2, 3, 6)
    S_BANKS = (0, 2, 6)
    SHIFT = 20
    with ExitStack() as ctx:
        s = Section(nc, ctx, "l2f")
        ps = ctx.enter_context(nc.psum_tensor("l2f_ps", [P, 8, BANK], F32))
        ln = LayerNorm(s, K, ps)
        wqkv = s.sb("wqkv", [P, KD, 3 * INNER])
        wo = s.sb("wo", [P, NP, D])
        w1 = s.sb("w1", [P, KD, 2 * F])
        w2 = s.sb("w2", [P, NF, D])
        wqkv_low = s.sb("wqkv_low", [P, KD, 3 * INNER], BF16)
        w1_low = s.sb("w1_low", [P, KD, 2 * F], BF16)
        w2_low = s.sb("w2_low", [P, NF, D], BF16)
        gb = s.sb("ln_gain_bias", [P, 2, KD])
        b1 = s.sb("b1", [P, 2, NF])
        b2 = s.sb("b2", [P, KD])
        qks = s.sb("qk_scales", [P, 2, hd])
        tab = s.sb("rotary", [P, 2, 2, NT, hd])
        masks, identb = K.masks, K.identb
        eps_norm = s.sb("eps_norm", [P, 1])
        xs = s.sb("xs", [P, KD, T])
        xs_low = s.sb("xs_low", [P, KD, T], BF16)
        xn = s.sb("xn_high", [P, KD, T])
        xn_low = s.sb("xn_low", [P, KD, T], BF16)
        sq = s.sb("qk_squares", [P, 2, BANK])
        tsn = s.sb("sin_part", [P, 2, BANK])
        ss = s.sb("sumsq", [P, 2, 4, 8])
        rn = s.sb("rnorm", [P, 2, 4, 8])
        tok = s.sb("by_token", [P, 2 * 2 * INNER])
        qT = s.sb("qT", [P, NP, T])
        kT = s.sb("kT", [P, NP, W + T])
        vt = s.sb("v_by_token", [P, NT, NP, 3, hd])
        mtok = s.sb("max_by_token", [P, NT, H])
        mT = s.sb("max_by_head", [H, NT, SK], BF16)
        gate = ln.rstd
        g = s.sb("hidden", [P, 2, T])
        g_low = s.sb("hidden_low", [P, 2, T], BF16)
        qTu, kTu = upper(qT[:, :, :]), upper(kT[:, :, :])
        zeros = kT[:, 0:(T - SK) // W, 0:W // 2].bitcast(BF16)
        prob = tok[:, 0:2 * NT * SK].rearrange("p (h t n) -> p h t n", h=2, t=NT)
        rec = tok[:, 2 * NT * SK:2 * NT * SK + T]
        SLOTS = 4
        slots = tok[:, 4 * INNER - SLOTS * BANK:4 * INNER].rearrange("p (s n) -> p s n", s=SLOTS)
        qk_tok = tok[:, :].rearrange("p (u n) -> p u n", u=2)

        cleared = s.sig("cleared")
        wo_loaded, ffn_loaded = s.sig("wo_loaded", 16), s.sig("ffn_vectors_loaded", 16 * 3)
        tab_loaded, tab_ready = s.sig("tables_loaded", 16 * 3), s.sig("tables_ready")
        tab_free = s.sig("tables_free", ahead=1)
        xs_high, xs_ready = s.sig("xs_high_ready"), s.sig("xs_ready")
        qkv_blocks = [("L2_ffn_Wqkv", wqkv, wqkv_low, P, slice(k, k + 1), slice(n * BANK, (n + 1) * BANK))
                      for k in range(KD) for n in range(3 * INNER // BANK)]
        ffn_blocks = [("L2_ffn_W1", w1, w1_low, P, slice(k, k + 1), slice(lo, min(lo + BANK, 2 * F)))
                      for k in range(KD) for lo in range(0, 2 * F, BANK)]
        ffn_blocks += [("L2_ffn_W2", w2, w2_low, P, slice(f, min(f + 2, NF - 1)), slice(0, D)) for f in range(0, NF - 1, 2)]
        ffn_blocks += [("L2_ffn_W2", w2, w2_low, FR, slice(NF - 1, NF), slice(0, D))]
        qkv_split = s.sig("wqkv_split", 2 * len(qkv_blocks))
        ffn_split = s.sig("ffn_weights_split", 2 * len(ffn_blocks))
        qkv_in = [s.sig(f"wqkv_slot{n}_loaded", 16 * len(qkv_blocks[n::SLOTS])) for n in range(SLOTS)]
        ffn_in = [s.sig(f"ffn_slot{n}_loaded", 16 * len(ffn_blocks[n::SLOTS])) for n in range(SLOTS)]
        qk_ready, sq_ready, qk_taken = s.sig("qk_ready", 16), s.sig("qk_squares_ready", 16), s.sig("qk_taken", 16)
        sum_ready, rope_ready = s.sig("sums_ready", 16), s.sig("rope_ready", 16)
        clamped, logn, rn_ready, tok_ready = s.sig("sums_clamped", NT), s.sig("log_norm", NT), s.sig("rnorm_ready", NT), s.sig("tok_ready", NT)
        v_ready, v_taken = s.sig("v_ready", 8), s.sig("v_taken", 8)
        turned, turn_taken = s.sig("qk_turned", 16), s.sig("qkT_ready", 16)
        s_ready, s_max = s.sig("scores_ready", H), s.sig("scores_maxed", H)
        mt_ready, mt_taken = s.sig("max_turned"), s.sig("max_taken", ahead=1)
        st_ready, p_ready = s.sig("scoresT_ready", H), s.sig("prob_ready", H)
        o_ready, rec_ready, o_norm = s.sig("out_ready", H), s.sig("recip_ready", H), s.sig("out_normed", H)
        rec_log = s.sig("denominator_log", H)
        y_ready, x_mid = s.sig("y_ready", ahead=1), s.sig("x_mid_ready")
        biased_ready, xn_high, xn_split = s.sig("xn_biased"), s.sig("xn_high_ready"), s.sig("xn_split")
        hidden, g_high = s.sig("hidden_ready", NF), s.sig("hidden_high_ready", NF)
        up_ready, gate_ready, g_ready = s.sig("up_ready", NF), s.sig("gate_ready", NF), s.sig("hidden_split", NF)
        z_ready, x_done = s.sig("z_ready"), s.sig("x_done", ahead=1)
        block = s.block()

        def steps(qkv, ffn):
            if not qkv:
                order = ["mean", "var", ("up", 0)]
                for f in range(1, NF):
                    order += [("up", f), ("down", f - 1)]
                return order + [("down", NF - 1)]
            between = {(0, 2): ["mean"], (0, 4): ["var"], (1, 1): [("up", 0)], (1, 5): [("up", 1)],
                       (2, 1): [("down", 0)], (2, 2): [("up", 2)], (2, 5): [("down", 1)],
                       (3, 0): [("up", 3)], (3, 2): [("down", 2)], (3, 4): [("up", 4)],
                       (3, 5): [("down", 3), ("up", 5), ("down", 4)]}
            order = []
            for t in range(NT):
                for i in range(6):
                    order.append(("project", t, i))
                    if t and i >= 2:
                        order.append(("turn", t - 1, i - 2))
                    if i == 5:
                        order.append(("norm", t))
                    if ffn:
                        order += between.get((t, i), [])
            last = [("turn", NT - 1, u) for u in range(4)]
            return order + (last[0:2] + [("down", 5)] + last[2:4] if ffn else last)

        assert NF == 6

        def turn_bank(t, u):
            return RING[0] if t == NT - 1 and u % 2 else 7

        def step(what):
            return (what,) if isinstance(what, str) else what

        @block.sync
        def _(sp):
            def load_block(l, n, block, loaded, split):
                name, _, _, rows, chunks, columns = block
                if n >= SLOTS:
                    sp.wait_ge(split.sem, split.at(l, 2 * (n - SLOTS) + 2))
                source = a[name][bass.ds(l, 1), chunks.start * P:(chunks.stop - 1) * P + rows, columns]
                width = (chunks.stop - chunks.start) * (columns.stop - columns.start)
                to = slots[0:rows, n % SLOTS, 0:width].rearrange("p (c n) -> p c n", c=chunks.stop - chunks.start)
                sp.dma_start(to, source.rearrange("l (c p) n -> p (l c) n", p=rows)).then_inc(loaded[n % SLOTS].sem, 16)

            with sp.Fori(0, DEPTH) as l:
                one = bass.ds(l, 1)
                sp.wait_ge(tab_free.sem, tab_free.at(l * B))
                sp.dma_start(tab[:, :, :, :, :], a["rotary"].rearrange("p (f g t d) -> p f g t d", f=2, g=2, t=NT))\
                    .then_inc(tab_loaded.sem, 16)
                for n, name in enumerate(("L2_ffn_q_scale", "L2_ffn_k_scale")):
                    sp.dma_start(qks[:, n, :], a[name][one, :].broadcast_to([P, hd])).then_inc(tab_loaded.sem, 16)
                sp.wait_ge(mt_taken.sem, mt_taken.at(l * B))
                for n, blk in enumerate(qkv_blocks):
                    load_block(l, n, blk, qkv_in, qkv_split)
                sp.wait_ge(y_ready.sem, y_ready.at(l * B))
                sp.dma_start(wo[:, :, :], a["L2_ffn_Wo"][one, :, :].rearrange("l (k p) n -> p (l k) n", p=P))\
                    .then_inc(wo_loaded.sem, 16)
                sp.wait_ge(x_done.sem, x_done.at(l * B))
                sp.dma_start(gb[:, :, :], a["ln_gain_bias"][one, :, :].rearrange("l p (g k) -> p (l g) k", g=2))\
                    .then_inc(ffn_loaded.sem, 16)
                sp.dma_start(b1[:, :, :], a["b1_columns"][one, :, :].rearrange("l p (g k) -> p (l g) k", g=2))\
                    .then_inc(ffn_loaded.sem, 16)
                sp.dma_start(b2[:, :], a["b2_columns"][one, :, :].rearrange("l p k -> p (l k)"))\
                    .then_inc(ffn_loaded.sem, 16)
                sp.wait_ge(mt_taken.sem, mt_taken.at(l * B, 1))
                for n, blk in enumerate(ffn_blocks):
                    load_block(l, n, blk, ffn_in, ffn_split)
            sp.wait_ge(ffn_loaded.sem, ffn_loaded.at(DEPTH))

        def x_of(k, it, first):
            return K.x[:, k, bass.ds(it % B, 1), first:first + T].rearrange("p a t -> p (a t)")

        def x_shifted(k, it):
            return x_of(k, it, 1 - k)

        @block.tensor
        def _(pe):
            y_ready.raise_ahead(pe)
            pe.wait_ge(cleared.sem, 1)

            def free_unit(nxt, n):
                t, i = n // 6, n % 6
                if UNITS[i] < 4:
                    pe.wait_ge(qk_taken.sem, qk_taken.at(nxt, 4 * t + UNITS[i] + 1))
                else:
                    pe.wait_ge(v_taken.sem, v_taken.at(nxt, 2 * t + UNITS[i] - 3))

            def project(nxt, t, i):
                n, u = 6 * t + i, UNITS[i]
                if n >= 3:
                    free_unit(nxt, n - 3)
                for k in range(KD):
                    tokens, columns = slice(t * P, (t + 1) * P), slice(u * BANK, (u + 1) * BANK)
                    ins = split_matmul(pe, ps[:, RING[n % 3], :], (xs[:, k, tokens], xs_low[:, k, tokens]),
                                       (wqkv[:, k, columns], wqkv_low[:, k, columns]), start=k == 0, stop=k == KD - 1)
                ins.then_inc(qk_ready.sem if u < 4 else v_ready.sem, 1)

            def turn(nxt, t, u):
                n = 4 * t + u
                if u == 0:
                    pe.wait_ge(tok_ready.sem, tok_ready.at(nxt, t + 1))
                bank = turn_bank(t, u)
                if bank == RING[0]:
                    free_unit(nxt, 21)
                if t < NT - 1 or u == 0:
                    before = n
                else:
                    before = n - 1
                if n and not (t == NT - 1 and u == 1):
                    pe.wait_ge(turn_taken.sem, turn_taken.at(nxt, before))
                for j in range(4):
                    ins = pe.transpose(ps[:, bank, j * P:(j + 1) * P], qk_tok[:, t % 2, u * BANK + j * P:u * BANK + (j + 1) * P],
                                       K.ident[:, :])
                ins.then_inc(turned.sem, 1)

            def attention(it):
                pe.wait_ge(qk_taken.sem, qk_taken.at(it, 16))
                pe.wait_ge(v_taken.sem, v_taken.at(it, 8))
                pe.wait_ge(turn_taken.sem, turn_taken.at(it, 16))
                for h in range(H):
                    rows, p = slice((h % 2) * hd, (h % 2 + 1) * hd), h // 2
                    if h >= 3:
                        pe.wait_ge(s_max.sem, s_max.at(it, h - 2))
                    for a2 in range(2):
                        bank = S_BANKS[h % 3] + a2
                        pe.matmul(ps[:, bank, 0:2 * SK], identb[:, :], masks[:, a2 * 2 * SK:(a2 + 1) * 2 * SK],
                                  start=True, stop=False)
                        for t2 in range(2):
                            t = 2 * a2 + t2
                            ins = pe.matmul(ps[:, bank, t2 * SK:(t2 + 1) * SK], qTu[rows, p, t * P:(t + 1) * P],
                                            kTu[rows, p, t * P:t * P + SK], start=False, stop=t2 == 1)
                    ins.then_inc(s_ready.sem, 1)
                pe.wait_ge(s_max.sem, s_max.at(it, H))
                pe.wait_ge(x_done.sem, x_done.at(it))
                for t in range(NT):
                    ins = pe.transpose(ps[0:H, 4, t * P:(t + 1) * P], mtok[:, t, :], K.ident[:, :])
                ins.then_inc(mt_ready.sem, 1)
                pe.wait_ge(mt_taken.sem, mt_taken.at(it, 1))

                def scoresT(h):
                    rows, p = slice((h % 2) * hd, (h % 2 + 1) * hd), h // 2
                    if h >= 2:
                        pe.wait_ge(p_ready.sem, p_ready.at(it, h - 1))
                    for a2 in range(2):
                        bank = 2 * (h % 2) + a2
                        pe.matmul(ps[:, bank, 0:2 * SK], identb[:, :], masks[:, 4 * SK:6 * SK], start=True, stop=False)
                        pe.matmul(ps[:, bank, 0:2 * SK], K.neg_of_head(h), mT[:, 2 * a2:2 * a2 + 2, :], start=False, stop=False)
                        for t2 in range(2):
                            t = 2 * a2 + t2
                            width = min(SK, T - t * P)
                            ins = pe.matmul(ps[:, bank, t2 * SK:t2 * SK + width], kT[rows, p, W + t * P:W + (t + 1) * P],
                                            qT[rows, p, t * P:t * P + width], start=False, stop=t2 == 1)
                    ins.then_inc(st_ready.sem, 1)

                def values(h):
                    pe.wait_ge(p_ready.sem, p_ready.at(it, h + 1))
                    if h >= 2:
                        pe.wait_ge(o_norm.sem, o_norm.at(it, h - 1))
                    for t in range(NT):
                        width = min(SK, T - t * P)
                        ins = pe.matmul(ps[:, 6 + h % 2, t * P:t * P + width], vt[:, t, h // 2, h % 2:h % 2 + 2, :],
                                        prob[:, h % 2, t, 0:width], start=t == 0, stop=t == NT - 1)
                        if t == 0:
                            pe.matmul(ps[:, 6 + h % 2, SK:T], identb[:, :], zeros, start=False, stop=False)
                    ins.then_inc(o_ready.sem, 1)

                def project_out(p):
                    pe.wait_ge(o_norm.sem, o_norm.at(it, 2 * p + 2))
                    for m in range(KD):
                        ins = pe.matmul(ps[:, 4 + m, :], wo[:, p, m * P:(m + 1) * P], qT[:, p, :],
                                        start=p == 0, stop=p == NP - 1)
                    return ins

                scoresT(0)
                pe.wait_ge(wo_loaded.sem, wo_loaded.at(it // B, 16))
                for h in range(H):
                    if h + 1 < H:
                        scoresT(h + 1)
                    values(h)
                    if h % 2 == 1 and h >= 3:
                        project_out(h // 2 - 1)
                project_out(NP - 1).then_inc(y_ready.sem, 1)

            def up(it, f):
                rows = P if f < NF - 1 else FR
                if f == 0:
                    pe.wait_ge(xn_split.sem, xn_split.at(it, 1))
                    pe.wait_ge(ffn_split.sem, ffn_split.at(it // B, ffn_split.per))
                else:
                    pe.wait_ge(g_ready.sem, g_ready.at(it, f))
                for half in (1, 0):
                    for k in range(KD):
                        columns = slice(half * F + f * P, half * F + f * P + rows)
                        ins = split_matmul(pe, ps[0:rows, 1 - half, :], (w1[:, k, columns], w1_low[:, k, columns]),
                                           (xn[:, k, :], xn_low[:, k, :]), start=k == 0, stop=k == KD - 1)
                ins.then_inc(up_ready.sem, 1)

            def down(it, f):
                rows = P if f < NF - 1 else FR
                pe.wait_ge(g_ready.sem, g_ready.at(it, f + 1))
                for m in range(KD):
                    columns = slice(m * P, (m + 1) * P)
                    ins = split_matmul(pe, ps[:, 4 + m, :], (w2[0:rows, f, columns], w2_low[0:rows, f, columns]),
                                       (g[0:rows, f % 2, :], g_low[0:rows, f % 2, :]), start=f == 0, stop=f == NF - 1)
                if f == NF - 1:
                    ins.then_inc(z_ready.sem, 1)

            def rest(it, nxt):
                if nxt is not None:
                    pe.wait_ge(xs_ready.sem, xs_ready.at(nxt, 1))
                    pe.wait_ge(qkv_split.sem, qkv_split.at(nxt // B, qkv_split.per))
                for name, *at in map(step, steps(nxt is not None, it is not None)):
                    if name == "project":
                        project(nxt, *at)
                    elif name == "turn":
                        turn(nxt, *at)
                    elif name == "mean":
                        pe.wait_ge(x_mid.sem, x_mid.at(it, 1))
                        ln.pe_mean(pe, lambda k: x_shifted(k, it))
                    elif name == "var":
                        ln.pe_var(pe, it)
                    elif name == "up":
                        up(it, *at)
                    elif name == "down":
                        down(it, *at)

            rest(None, 0)
            with pe.Fori(0, PASSES - 1) as it:
                attention(it)
                rest(it, it + 1)
            attention(PASSES - 1)
            rest(PASSES - 1, None)

        @block.vector
        def _(dve):
            x_done.raise_ahead(dve)
            mt_taken.raise_ahead(dve)
            dve.memset(kT[:, :, 0:W], 0.0)
            dve.memset(vt[:, :, :, 1, :], 1.0)
            dve.memset(mT[:, NT - 1, P:SK], 0.0)
            dve.memset(eps_norm[:, :], SHIFT / 2 * 0.6931471805599453).then_inc(cleared.sem, 1)
            tab_free.raise_ahead(dve)

            def scale_tables(l):
                dve.wait_ge(tab_loaded.sem, tab_loaded.at(l, tab_loaded.per))
                for n in range(2):
                    for trig, lo, hi in ((0, 0, hd), (1, HALF, hd), (1, 0, HALF)):
                        at = slice(0, hd) if trig == 0 else slice(HALF - lo, hd - lo)
                        part = tab[:, n, trig, :, at]
                        ins = dve.tensor_tensor(part, part, qks[:, n:n + 1, lo:hi].broadcast_to([P, NT, hi - lo]), ALU.mult)
                ins.then_inc(tab_ready.sem, 1)

            def high(out, x):
                return dve.tensor_scalar(out.bitcast(F32R), x, 1.0, None, ALU.mult)

            def split_block(l, n, block, loaded, done):
                _, w, low, rows, chunks, columns = block
                w, low = w[0:rows, chunks, columns], low[0:rows, chunks, columns]
                c, width = w.shape[1], w.shape[2]
                raw = slots[0:rows, n % SLOTS, 0:c * width].rearrange("p (c n) -> p c n", c=c)
                dve.wait_ge(loaded[n % SLOTS].sem, loaded[n % SLOTS].at(l, 16 * (n // SLOTS + 1)))
                high(w, raw).then_inc(done.sem, 1)
                dve.wait_ge(done.sem, done.at(l, 2 * n + 1))
                dve.tensor_tensor(low, raw, w, ALU.subtract).then_inc(done.sem, 1)

            def stage(nxt):
                for k in range(KD):
                    ins = high(xs[:, k, :], x_shifted(k, nxt))
                ins.then_inc(xs_high.sem, 1)
                dve.wait_ge(xs_high.sem, xs_high.at(nxt, 1))
                for k in range(KD):
                    ins = dve.tensor_tensor(xs_low[:, k, :], x_shifted(k, nxt), xs[:, k, :], ALU.subtract)
                ins.then_inc(xs_ready.sem, 1)

            def rotate(nxt, t, u):
                n = 4 * t + u
                dve.wait_ge(sq_ready.sem, sq_ready.at(nxt, n + 1))
                if n >= 2:
                    dve.wait_ge(rope_ready.sem, rope_ready.at(nxt, n - 1))
                bank = RING[(6 * t + UNITS.index(u)) % 3]
                part = ps[:, bank, :].rearrange("p (h d) -> p h d", d=hd)
                cos = tab[:, u // 2, 0, t:t + 1, :].broadcast_to([P, 8, hd])
                if t >= 2 and u == 0:
                    dve.wait_ge(turned.sem, turned.at(nxt, 4 * (t - 1)))
                to = qk_tok[:, t % 2, u * BANK:(u + 1) * BANK].rearrange("p (h d) -> p h d", d=hd)
                dve.tensor_tensor(to, part, cos, ALU.mult)
                sn = tsn[:, n % 2, :].rearrange("p (h d) -> p h d", d=hd)
                for lo, src in ((0, HALF), (HALF, 0)):
                    sin = tab[:, u // 2, 1, t:t + 1, lo:lo + HALF].broadcast_to([P, 8, HALF])
                    ins = dve.tensor_tensor(sn[:, :, lo:lo + HALF], part[:, :, src:src + HALF], sin, ALU.mult)
                ins.then_inc(qk_taken.sem, 1)
                dve.tensor_reduce(ss[:, t % 2, u, :], sq[:, n % 2, :].rearrange("p (h d) -> p h d", d=hd),
                                  AX.X, ALU.add).then_inc(sum_ready.sem, 1)

            def attention(it, nxt, qkv_of=None, ffn_of=None):
                if qkv_of is not None:
                    scale_tables(qkv_of)
                for h in range(H):
                    dve.wait_ge(s_ready.sem, s_ready.at(it, h + 1))
                    base = S_BANKS[h % 3]
                    dve.tensor_reduce(mtok[:, :, h], ps[:, base:base + 2, 0:2 * SK].rearrange("p a (t n) -> p a t n", n=SK),
                                      AX.X, ALU.max).then_inc(s_max.sem, 1)
                dve.wait_ge(mt_ready.sem, mt_ready.at(it, 1))
                by_tile = ps[0:H, 4, :].rearrange("h (t n) -> h t n", t=NT)
                dve.tensor_copy(mT[:, :, 0:P], by_tile)
                dve.tensor_copy(mT[:, 0:NT - 1, P:SK], by_tile[:, 1:NT, 0:W]).then_inc(mt_taken.sem, 1)
                if nxt is not None:
                    dve.wait_ge(x_done.sem, x_done.at(it))
                    stage(nxt)
                for h in range(H):
                    if qkv_of is not None and h < len(qkv_blocks):
                        split_block(qkv_of, h, qkv_blocks[h], qkv_in, qkv_split)
                    if ffn_of is not None and 0 <= h - FFN_FROM < len(ffn_blocks):
                        split_block(ffn_of, h - FFN_FROM, ffn_blocks[h - FFN_FROM], ffn_in, ffn_split)
                    own = slice((h % 2) * hd, (h % 2 + 1) * hd)
                    dve.wait_ge(rec_ready.sem, rec_ready.at(it, h + 1))
                    dve.tensor_tensor(qT[own, h // 2, :], ps[own, 6 + h % 2, :], rec[own, :], ALU.mult)\
                        .then_inc(o_norm.sem, 1)
                dve.wait_ge(y_ready.sem, y_ready.at(it, 1))
                for m in range(KD):
                    xm = x_of(m, it, 1)
                    ins = dve.tensor_tensor(xm, ps[:, 4 + m, :], xm, ALU.add)
                ins.then_inc(x_mid.sem, 1)

            def rest(it, nxt):
                if nxt is not None:
                    dve.wait_ge(tab_ready.sem, tab_ready.at(nxt // B, 1))
                for name, *at in map(step, steps(nxt is not None, it is not None)):
                    if name == "project" and UNITS[at[1]] < 4:
                        rotate(nxt, at[0], UNITS[at[1]])
                    elif name == "norm":
                        t = at[0]
                        dve.wait_ge(sum_ready.sem, sum_ready.at(nxt, 4 * t + 4))
                        dve.tensor_scalar(ss[:, t % 2, :, :], ss[:, t % 2, :, :], 1e-24, None, ALU.max).then_inc(clamped.sem, 1)
                        if t == NT - 1:
                            dve.wait_ge(qk_taken.sem, qk_taken.at(nxt, 16))
                            dve.sem_inc(tab_free.sem, 1)
                    elif name == "mean":
                        dve.wait_ge(x_mid.sem, x_mid.at(it, 1))
                        dve.wait_ge(ln.mean_ready.sem, ln.mean_ready.at(it, 1))
                        for k in range(KD):
                            ins = dve.tensor_tensor(ln.xc[:, k, :], x_shifted(k, it), ps[:, 0, :], ALU.subtract)
                        ins.then_inc(ln.centered_ready.sem, 1)
                    elif name == "var":
                        dve.wait_ge(ffn_loaded.sem, ffn_loaded.at(it // B, ffn_loaded.per))
                        dve.wait_ge(ln.rstd_ready.sem, ln.rstd_ready.at(it, 1))
                        for k in range(KD):
                            ins = dve.scalar_tensor_tensor(out=ln.xc[:, k, :], in0=ln.xc[:, k, :], scalar=gb[:, 0, k:k + 1],
                                                           in1=ln.rstd[:, :], op0=ALU.mult, op1=ALU.mult)
                        ins.then_inc(ln.xn_ready.sem, 1)
                        dve.wait_ge(ln.xn_ready.sem, ln.xn_ready.at(it, 1))
                        for k in range(KD):
                            ins = dve.tensor_scalar(ln.xc[:, k, :], ln.xc[:, k, :], gb[:, 1, k:k + 1], None, ALU.add)
                        ins.then_inc(biased_ready.sem, 1)
                        dve.wait_ge(biased_ready.sem, biased_ready.at(it, 1))
                        for k in range(KD):
                            ins = high(xn[:, k, :], ln.xc[:, k, :])
                        ins.then_inc(xn_high.sem, 1)
                        dve.wait_ge(xn_high.sem, xn_high.at(it, 1))
                        for k in range(KD):
                            ins = dve.tensor_tensor(xn_low[:, k, :], ln.xc[:, k, :], xn[:, k, :], ALU.subtract)
                        ins.then_inc(xn_split.sem, 1)
                    elif name == "up":
                        f = at[0]
                        rows = P if f < NF - 1 else FR
                        dve.wait_ge(up_ready.sem, up_ready.at(it, f + 1))
                        dve.wait_ge(gate_ready.sem, gate_ready.at(it, f + 1))
                        dve.scalar_tensor_tensor(out=gate[0:rows, :], in0=ps[0:rows, 1, :], scalar=b1[0:rows, 0, f:f + 1],
                                                 in1=gate[0:rows, :], op0=ALU.add, op1=ALU.mult).then_inc(hidden.sem, 1)
                        dve.wait_ge(hidden.sem, hidden.at(it, f + 1))
                        high(g[0:rows, f % 2, :], gate[0:rows, :]).then_inc(g_high.sem, 1)
                        dve.wait_ge(g_high.sem, g_high.at(it, f + 1))
                        dve.tensor_tensor(g_low[0:rows, f % 2, :], gate[0:rows, :], g[0:rows, f % 2, :], ALU.subtract)\
                            .then_inc(g_ready.sem, 1)
                    elif name == "down" and at[0] == NF - 1:
                        dve.wait_ge(z_ready.sem, z_ready.at(it, 1))
                        for m in range(KD):
                            xm = x_of(m, it, 1)
                            ins = dve.scalar_tensor_tensor(out=xm, in0=ps[:, 4 + m, :], scalar=b2[:, m:m + 1], in1=xm,
                                                           op0=ALU.add, op1=ALU.add)
                        ins.then_inc(x_done.sem, 1)

            scale_tables(0)
            stage(0)
            for n, blk in enumerate(qkv_blocks):
                split_block(0, n, blk, qkv_in, qkv_split)
            rest(None, 0)

            def first_three(l):
                attention(l * B, l * B + 1, ffn_of=l)
                rest(l * B, l * B + 1)
                with dve.Fori(1, B - 1) as b:
                    attention(l * B + b, l * B + b + 1)
                    rest(l * B + b, l * B + b + 1)

            with dve.Fori(0, DEPTH - 1) as l:
                first_three(l)
                attention(l * B + B - 1, l * B + B, qkv_of=l + 1)
                rest(l * B + B - 1, l * B + B)
            first_three(DEPTH - 1)
            attention(PASSES - 1, None)
            rest(PASSES - 1, None)

        @block.gpsimd
        def _(pool):
            def rest(nxt):
                for t in range(NT):
                    for u in range(4):
                        n = 4 * t + u
                        pool.wait_ge(qk_taken.sem, qk_taken.at(nxt, n + 1))
                        part = qk_tok[:, t % 2, u * BANK:(u + 1) * BANK]
                        pool.tensor_tensor(part, part, tsn[:, n % 2, :], ALU.add).then_inc(rope_ready.sem, 1)
                    pool.wait_ge(rope_ready.sem, rope_ready.at(nxt, 4 * t + 4))
                    pool.wait_ge(rn_ready.sem, rn_ready.at(nxt, t + 1))
                    view = qk_tok[:, t % 2, :].rearrange("p (h d) -> p h d", d=hd)
                    r = rn[:, t % 2, :, :].rearrange("p u (h e) -> p (u h) e", e=1).broadcast_to([P, 32, hd])
                    pool.tensor_tensor(view, view, r, ALU.mult).then_inc(tok_ready.sem, 1)

            rest(0)
            with pool.Fori(0, PASSES - 1) as it:
                rest(it + 1)

        @block.scalar
        def _(act):
            act.wait_ge(cleared.sem, 1)

            def project(nxt, t, i):
                bank, u = ps[:, RING[(6 * t + i) % 3], :], UNITS[i]
                if u < 4:
                    n = 4 * t + u
                    act.wait_ge(qk_ready.sem, qk_ready.at(nxt, n + 1))
                    if n >= 2:
                        act.wait_ge(sum_ready.sem, sum_ready.at(nxt, n - 1))
                    act.activation(sq[:, n % 2, :], bank, ACT.Square).then_inc(sq_ready.sem, 1)
                    return
                v = u - 4
                act.wait_ge(v_ready.sem, v_ready.at(nxt, 2 * t + v + 1))
                act.activation(vt[:, t, 4 * v:4 * v + 4, 0:3:2, :], bank.rearrange("p (j g d) -> p j g d", g=2, d=hd),
                               ACT.Copy).then_inc(v_taken.sem, 1)

            def norm(nxt, t):
                act.wait_ge(clamped.sem, clamped.at(nxt, t + 1))
                act.activation(rn[:, t % 2, :, :], ss[:, t % 2, :, :], ACT.Ln, scale=2.0 ** SHIFT).then_inc(logn.sem, 1)
                act.wait_ge(logn.sem, logn.at(nxt, t + 1))
                act.activation(rn[:, t % 2, :, :], rn[:, t % 2, :, :], ACT.Exp, scale=-0.5, bias=eps_norm[:, :])\
                    .then_inc(rn_ready.sem, 1)

            def turn(nxt, t, u):
                act.wait_ge(turned.sem, turned.at(nxt, 4 * t + u + 1))
                src = ps[:, turn_bank(t, u), :].rearrange("p (j n) -> p j n", j=4)
                j = 4 * (u % 2)
                if u < 2:
                    dst = qT[:, j:j + 4, t * P:(t + 1) * P]
                else:
                    dst = kT[:, j:j + 4, W + t * P:W + (t + 1) * P]
                act.activation(dst, src, ACT.Copy).then_inc(turn_taken.sem, 1)

            def attention(it):
                def exponentials(h):
                    act.wait_ge(st_ready.sem, st_ready.at(it, h + 1))
                    if h >= 2:
                        act.wait_ge(o_ready.sem, o_ready.at(it, h - 1))
                    act.activation(prob[:, h % 2, :, :], ps[:, 2 * (h % 2):2 * (h % 2) + 2, 0:2 * SK], ACT.Exp,
                                   scale=QK_SCALE).then_inc(p_ready.sem, 1)

                def reciprocals(h):
                    own = slice((h % 2) * hd, (h % 2 + 1) * hd)
                    other = slice((1 - h % 2) * hd, (2 - h % 2) * hd)
                    act.wait_ge(o_ready.sem, o_ready.at(it, h + 1))
                    if h >= 2:
                        act.wait_ge(o_norm.sem, o_norm.at(it, h - 1))
                    act.activation(rec[own, :], ps[other, 6 + h % 2, :], ACT.Ln).then_inc(rec_log.sem, 1)
                    act.wait_ge(rec_log.sem, rec_log.at(it, h + 1))
                    act.activation(rec[own, :], rec[own, :], ACT.Exp, scale=-1.0).then_inc(rec_ready.sem, 1)

                exponentials(0)
                for h in range(H):
                    if h + 1 < H:
                        exponentials(h + 1)
                    reciprocals(h)

            def rest(it, nxt):
                gelu_last = False
                for name, *at in map(step, steps(nxt is not None, it is not None)):
                    if name == "project":
                        project(nxt, *at)
                    elif name == "turn":
                        turn(nxt, *at)
                    elif name == "norm":
                        if gelu_last:
                            act.preload_act_table_set("natural_log_exp_and_others")
                            gelu_last = False
                        norm(nxt, *at)
                    elif name == "mean":
                        ln.act_squares(act, it)
                    elif name == "var":
                        ln.act_rstd(act, it)
                    elif name == "up":
                        f = at[0]
                        rows = P if f < NF - 1 else FR
                        act.wait_ge(up_ready.sem, up_ready.at(it, f + 1))
                        act.activation(gate[0:rows, :], ps[0:rows, 0, :], ACT.Gelu, bias=b1[0:rows, 1, f:f + 1])\
                            .then_inc(gate_ready.sem, 1)
                        gelu_last = True

            act.preload_act_table_set("natural_log_exp_and_others")
            rest(None, 0)
            with act.Fori(0, PASSES - 1) as it:
                act.preload_act_table_set("natural_log_exp_and_others")
                attention(it)
                rest(it, it + 1)
            act.preload_act_table_set("natural_log_exp_and_others")
            attention(PASSES - 1)
            rest(PASSES - 1, None)


def mole(nc, K, a):
    E, R, HID = 3, 8, 1024
    NH = HID // P
    ER = E * R
    AR = ER + E
    TS = 32
    with ExitStack() as ctx:
        s = Section(nc, ctx, "l0f")
        ps = ctx.enter_context(nc.psum_tensor("l0f_ps", [P, 8, BANK], F32))
        ln = LayerNorm(s, K, ps)
        w1 = s.sb("w1", [P, KD, HID])
        w2 = s.sb("w2", [P, NH, D])
        ar1 = s.sb("a1_r1", [P, KD, AR])
        ar2 = s.sb("a2_r2", [P, NH, AR])
        lb1 = s.sb("lora_b1", [ER, HID])
        lb2 = s.sb("lora_b2", [ER, D])
        b1 = s.sb("b1", [P, NH])
        b2 = s.sb("b2", [P, KD])
        h = s.sb("hidden", [P, NH, T])
        top = s.sb("gate_max", [P, NT])
        e = s.sb("gates", [P, NT, E])
        den = s.sb("gate_sum", [P, NT])
        zg = s.sb("gated", [P, NT, ER])
        zgT = s.sb("gatedT", [ER, T])
        loaded = s.sig("loaded", 16 * 8)
        zr_ready, e_in, e_ready = s.sig("lowrank_ready", 2), s.sig("gate_logits_ready", 2), s.sig("gate_exp_ready", 2)
        zg_ready, zt_ready, zgT_ready = s.sig("gated_ready", 2), s.sig("gated_turned", 2), s.sig("gatedT_ready", 2)
        h_ready, h_taken = s.sig("hidden_ready", NH), s.sig("hidden_taken", NH)
        y_ready, x_done = s.sig("y_ready"), s.sig("x_done", ahead=1)
        dve_step = s.sig("dve_step", 2 * 4)
        block = s.block()

        @block.sync
        def _(sp):
            for dst, src in ((w1[:, :, :], a["L0_ffn_W1"].rearrange("(k p) n -> p k n", p=P)),
                             (ar1[:, :, :], a["L0_ffn_AR1"].rearrange("(k p) n -> p k n", p=P)),
                             (lb1[:, :], a["L0_ffn_B1"].rearrange("e r n -> (e r) n")),
                             (lb2[:, :], a["L0_ffn_B2"].rearrange("e r n -> (e r) n")),
                             (b1[:, :], a["L0_ffn_b1"]), (b2[:, :], a["L0_ffn_b2"]),
                             (ar2[:, :, :], a["L0_ffn_AR2"].rearrange("(k p) n -> p k n", p=P)),
                             (w2[:, :, :], a["L0_ffn_W2"].rearrange("(k p) n -> p k n", p=P))):
                sp.dma_start(dst, src).then_inc(loaded.sem, 16)
            sp.wait_ge(loaded.sem, loaded.per)

        @block.tensor
        def _(pe):
            with pe.Fori(0, B) as it:
                pe.wait_ge(x_done.sem, x_done.at(it))
                ln.pe_mean(pe, lambda k: K.x[:, k, bass.ds(it, 1), 1:T + 1])
                ln.pe_var(pe, it)
                pe.wait_ge(ln.xn_ready.sem, ln.xn_ready.at(it, 1))
                pe.wait_ge(loaded.sem, loaded.per)

                def low_rank(n, src, chunks, w):
                    for t in range(NT):
                        for k in range(chunks):
                            ins = pe.matmul(ps[:, 2, t * TS:t * TS + AR], src[:, k, t * P:(t + 1) * P], w[:, k, :],
                                            start=k == 0, stop=k == chunks - 1)
                    ins.then_inc(zr_ready.sem, 1)

                def turn_gated(n):
                    pe.wait_ge(zg_ready.sem, zg_ready.at(it, n + 1))
                    for t in range(NT):
                        ins = pe.transpose(ps[0:ER, 3, t * P:(t + 1) * P], zg[:, t, :], K.ident[:, :])
                    ins.then_inc(zt_ready.sem, 1)

                low_rank(0, ln.xn, KD, ar1)
                for c in range(NH):
                    if c >= 3:
                        pe.wait_ge(h_taken.sem, h_taken.at(it, c - 2))
                    for k in range(KD):
                        pe.matmul(ps[:, 4 + c % 3, :], w1[:, k, c * P:(c + 1) * P], ln.xn[:, k, :], start=k == 0, stop=False)
                    if c == 0:
                        turn_gated(0)
                        pe.wait_ge(zgT_ready.sem, zgT_ready.at(it, 1))
                    pe.matmul(ps[:, 4 + c % 3, :], lb1[:, c * P:(c + 1) * P], zgT[:, :], start=False, stop=True)\
                        .then_inc(h_ready.sem, 1)
                pe.wait_ge(h_taken.sem, h_taken.at(it, NH))
                low_rank(1, h, NH, ar2)
                for m in range(KD):
                    for c in range(NH):
                        pe.matmul(ps[:, 4 + m, :], w2[:, c, m * P:(m + 1) * P], h[:, c, :], start=c == 0, stop=False)
                turn_gated(1)
                pe.wait_ge(zgT_ready.sem, zgT_ready.at(it, 2))
                for m in range(KD):
                    ins = pe.matmul(ps[:, 4 + m, :], lb2[:, m * P:(m + 1) * P], zgT[:, :], start=False, stop=True)
                ins.then_inc(y_ready.sem, 1)

        @block.vector
        def _(dve):
            x_done.raise_ahead(dve)
            with dve.Fori(0, B) as it:
                dve.wait_ge(x_done.sem, x_done.at(it))
                step = Chain(dve, dve_step, it)
                ln.dve_center(dve, it, K.x[:, :, bass.ds(it, 1), 1:T + 1])
                ln.dve_scale(dve, it)
                dve.wait_ge(loaded.sem, loaded.per)
                for n in range(2):
                    tiles = ps[:, 2, 0:NT * TS].rearrange("p (t n) -> p t n", n=TS)

                    def wide(v):
                        return v.rearrange("p (t e) -> p t e", e=1).broadcast_to([P, NT, E])

                    dve.wait_ge(zr_ready.sem, zr_ready.at(it, n + 1))
                    step(dve.tensor_reduce(top[:, :], tiles[:, :, ER:AR], AX.X, ALU.max))
                    dve.tensor_tensor(e[:, :, :], tiles[:, :, ER:AR], wide(top[:, :]), ALU.subtract).then_inc(e_in.sem, 1)
                    dve.wait_ge(e_ready.sem, e_ready.at(it, n + 1))
                    step(dve.tensor_reduce(den[:, :], e[:, :, :], AX.X, ALU.add))
                    step(dve.reciprocal(den[:, :], den[:, :]))
                    step(dve.scalar_tensor_tensor(out=e[:, :, :], in0=e[:, :, :], scalar=1.0 / R, in1=wide(den[:, :]),
                                                  op0=ALU.mult, op1=ALU.mult))
                    for t in range(NT):
                        gates = e[:, t, :].rearrange("p (e r) -> p e r", r=1).broadcast_to([P, E, R])
                        ins = dve.tensor_tensor(zg[:, t, :].rearrange("p (e r) -> p e r", r=R),
                                                tiles[:, t, 0:ER].rearrange("p (e r) -> p e r", r=R), gates, ALU.mult)
                    ins.then_inc(zg_ready.sem, 1)
                step.end()
                dve.wait_ge(y_ready.sem, y_ready.at(it, 1))
                for m in range(KD):
                    xm = K.x[:, m, bass.ds(it, 1), 1:T + 1].rearrange("p a t -> p (a t)")
                    ins = dve.scalar_tensor_tensor(out=xm, in0=ps[:, 4 + m, :], scalar=b2[:, m:m + 1], in1=xm,
                                                   op0=ALU.add, op1=ALU.add)
                ins.then_inc(x_done.sem, 1)

        @block.scalar
        def _(act):
            act.preload_act_table_set("natural_log_exp_and_others")
            with act.Fori(0, B) as it:
                ln.act_squares(act, it)
                ln.act_rstd(act, it)
                act.wait_ge(loaded.sem, loaded.per)
                for n in range(2):
                    act.wait_ge(e_in.sem, e_in.at(it, n + 1))
                    act.activation(e[:, :, :], e[:, :, :], ACT.Exp).then_inc(e_ready.sem, 1)
                    act.wait_ge(zt_ready.sem, zt_ready.at(it, n + 1))
                    act.activation(zgT[:, :], ps[0:ER, 3, :], ACT.Copy).then_inc(zgT_ready.sem, 1)
                    if n == 0:
                        for c in range(NH):
                            act.wait_ge(h_ready.sem, h_ready.at(it, c + 1))
                            act.activation(h[:, c, :], ps[:, 4 + c % 3, :], ACT.Relu, bias=b1[:, c:c + 1])\
                                .then_inc(h_taken.sem, 1)


def shape_constants():
    import numpy as np

    c = {"ident": np.eye(128, dtype=np.float32)}
    rows = [(np.arange(128) // hd == j) for hd in (64, 32, 16) for j in range(128 // hd)]
    c["headrows"] = np.stack(rows, 1).astype(np.float32)
    c["index_before"] = (np.arange(8)[None, :] < np.arange(8)[:, None]).astype(np.float32).reshape(-1)
    c["pick"] = np.repeat(np.eye(8, dtype=np.float32), 128, 1).reshape(8, 1024)
    q, key = np.arange(128)[:, None], np.arange(192)[None, :]
    seen = (key <= q + 64) & (key >= q)
    by_token = [np.where(seen & ((key >= 64) | (t > 0)), 0.0, -1e30) for t in range(4)]
    key, q = np.arange(128)[:, None], np.arange(192)[None, :]
    by_key = [np.where((key <= q) & (key >= q - 64), 0.0, -1e30)] * 2
    c["masks"] = np.concatenate(by_token + by_key, 1).astype(np.float32)
    f = np.float32
    half = np.arange(0, 64, 2, dtype=f)
    inv_freq = f(1.0) / f(10000.0) ** (half / f(64))
    t = np.arange(512, dtype=f)
    freqs = t[:, None] * inv_freq[None, :]
    base = (half + f(0.4 * 64)) / f(1.4 * 64)
    power = (t - f(256)) / f(32)
    scale = (base[None, :].astype(np.float64) ** power[:, None]).astype(f)
    cos, sin = np.cos(freqs.astype(np.float64)).astype(f), np.sin(freqs.astype(np.float64)).astype(f)
    tables = []
    for sc in (scale, f(1.0) / scale):
        tables.append(np.concatenate([cos * sc, cos * sc], 1))
        tables.append(np.concatenate([-sin * sc, sin * sc], 1))
    r = np.stack(tables).reshape(4, 4, 128, 64)
    c["rotary"] = np.ascontiguousarray(r.transpose(2, 0, 1, 3)).reshape(128, 1024)
    return c


class Constants:

    def __init__(self, nc, ctx):
        def sb(name, shape, dt=F32):
            return ctx.enter_context(nc.sbuf_tensor(name, shape, dt))

        self.x = sb("x", [P, KD, B, T + 1])
        self.ctxT = sb("ctxT", [P, 2, B, KEYS])
        self.mean = sb("mean_matrix", [P, P])
        self.eps = sb("eps", [P, 1])
        self.one = sb("one", [P, 1])
        self.ident = sb("ident", [P, P])
        self.headrows = sb("headrows", [P, 14])
        self.identb = sb("ident_bf16", [P, P], BF16)
        self.negident = sb("negident", [16, 16], BF16)
        self.masks = sb("masks", [P, 6 * 192], BF16)

    def neg_of_head(self, h):
        return self.negident[:, h:h + 1].broadcast_to([16, P])

    def rows(self, hd, j):
        at = {64: 0, 32: 2, 16: 6}[hd] + j
        return self.headrows[:, at:at + 1]


def load_constants(nc, K, a):
    with ExitStack() as ctx:
        s = Section(nc, ctx, "start")
        loaded = s.sig("constants_loaded").sem
        mask = s.sb("masks_f32", [P, 6 * 192])
        block = s.block()

        @block.sync
        def _(sp):
            n = 0
            for k in range(KD):
                sp.dma_start(K.x[:, k, :, 1:T + 1], a["xT"][k * P:(k + 1) * P, :].rearrange("p (b t) -> p b t", b=B))\
                    .then_inc(loaded, 16)
                n += 16
            for dst, src in ((K.ctxT[:, :, :, :], a["ctxT"].rearrange("(k p) (b n) -> p k b n", p=P, b=B)),
                             (K.ident[:, :], a["ident"]), (K.headrows[:, :], a["headrows"]),
                             (mask[:, :], a["masks"])):
                sp.dma_start(dst, src).then_inc(loaded, 16)
                n += 16
            sp.wait_ge(loaded, n)

        @block.vector
        def _(dve):
            dve.memset(K.mean[:, :], 1.0 / D)
            dve.memset(K.eps[:, :], EPS)
            dve.memset(K.one[:, :], 1.0)
            dve.memset(K.x[:, :, :, 0:1], 0.0)
            dve.wait_ge(loaded, 16 * (KD + 4))
            dve.tensor_copy(K.identb[:, :], K.ident[:, :])
            dve.tensor_scalar(K.negident[:, :], K.ident[0:16, 0:16], -1.0, None, ALU.mult)
            dve.tensor_copy(K.masks[:, :], mask[:, :])


def store_x(nc, K, out):
    with ExitStack() as ctx:
        s = Section(nc, ctx, "end")
        stored = s.sig("x_stored").sem
        block = s.block()

        @block.sync
        def _(sp):
            for k in range(KD):
                sp.dma_start(out[k * P:(k + 1) * P, :].rearrange("p (b t) -> p b t", b=B), K.x[:, k, :, 1:T + 1])\
                    .then_inc(stored, 16)
            sp.wait_ge(stored, 16 * KD)


def program(nc, a, out, stop=8):
    with ExitStack() as ctx:
        K = Constants(nc, ctx)
        load_constants(nc, K, a)
        no = None
        saved = nc.dram_tensor("x_saved", [D, B * T], F32).ap()
        stages = [
            lambda: cross_attention(nc, K, "l0x", 16, 64, dict(
                wq=a["L0_xattn_w_q"], wk=a["L0_xattn_w_k"], wv=a["L0_xattn_w_v"], wo=a["L0_xattn_w_out"],
                bo=a["L0_xattn_b_out"], bq=no), scale=64 ** -0.5),
            lambda: mole(nc, K, a),
            lambda: cross_attention(nc, K, "l1x", 8, 32, dict(
                wq=a["L1_xattn_Wq"], wk=a["L1_xattn_Wk"], wv=a["L1_xattn_Wv"], wo=a["L1_xattn_Wo"],
                bq=a["L1_xattn_bq"], bk=a["L1_xattn_bk"], bv=a["L1_xattn_bv"], bo=a["L1_xattn_bo"]), scale=32 ** -0.5),
            lambda: bitnet(nc, K, a),
            lambda: cross_attention(nc, K, "l2x", 16, 16, dict(
                wq=a["L2_xattn_Wq"], wk=a["L2_xattn_Wk"], wv=a["L2_xattn_Wv"], w1=a["L2_xattn_W1"],
                w2=a["L2_xattn_W2"], b1=a["L2_xattn_b1"], bq=a["L2_xattn_bq"], bk=a["L2_xattn_bk"],
                bv=a["L2_xattn_bv"], bo=a["L2_xattn_b2"]), scale=16 ** -0.5, ffn=True),
            lambda: (enter_inner_stream(nc, K, saved), local_transformer(nc, K, a), leave_inner_stream(nc, K, saved)),
            lambda: cross_attention(nc, K, "l3x", 16, 16, dict(
                wq=a["L3_xattn_Wq"], wk=a["L3_xattn_Wk"], wv=a["L3_xattn_Wv"], wo=a["L3_xattn_Wo"],
                bq=a["L3_xattn_bq"], bk=a["L3_xattn_bk"], bv=a["L3_xattn_bv"], bo=a["L3_xattn_bo"]),
                scale_in=a["L3_xattn_scale"]),
            lambda: experts(nc, K, a),
        ]
        for stage in stages[START:stop]:
            stage()
        store_x(nc, K, out)


START, STOP = 0, 8


def kernel(**inputs):
    import numpy as _np
    import concourse.bacc as _bacc
    from concourse import mybir as _mybir
    from concourse.bass_utils import run_bass_kernel_spmd as _run

    f32 = _np.float32
    arrays = {}
    for name, value in inputs.items():
        value = _np.asarray(value)
        if name == "x":
            arrays["xT"] = _np.ascontiguousarray(value.reshape(-1, value.shape[-1]).T)
        elif name == "ctx_768":
            flat = value.reshape(-1, value.shape[-1]).T
            arrays["ctxT"] = _np.concatenate([flat, _np.zeros((256 - flat.shape[0], flat.shape[1]), f32)])
        elif name.startswith("L1_xattn_W") or name in ("L1_ffn_w1", "L1_ffn_w2", "L3_ffn_routing_W"):
            arrays[name] = _np.ascontiguousarray(value.T)
        elif value.ndim == 1 and value.size % 128 == 0:
            arrays[name] = _np.ascontiguousarray(value.reshape(-1, 128).T)
        else:
            arrays[name] = _np.ascontiguousarray(value)
    for n in "12":
        down = arrays.pop(f"L0_ffn_A{n}").transpose(1, 0, 2)
        arrays[f"L0_ffn_AR{n}"] = _np.concatenate([down.reshape(down.shape[0], -1), arrays.pop(f"L0_ffn_R{n}")], 1)
    arrays["L3_ffn_rb1"] = _np.ascontiguousarray(arrays["L3_ffn_rb1"].T)
    conv = arrays.pop("L1_ffn_conv_w").reshape(8, 128, 3)
    arrays["conv_w_columns"] = _np.ascontiguousarray(conv.transpose(1, 0, 2)).reshape(128, 24)
    columns = lambda v: v.reshape(v.shape[0], -1, 128).transpose(0, 2, 1)
    pad = _np.zeros((6, 768 - 682), f32)
    b1 = arrays.pop("L2_ffn_b1")
    arrays["b1_columns"] = _np.concatenate([columns(_np.concatenate([h, pad], 1)) for h in (b1[:, :682], b1[:, 682:])], 2)
    arrays["ln_gain_bias"] = _np.concatenate([columns(arrays.pop("L2_ffn_ln_g")), columns(arrays.pop("L2_ffn_ln_b"))], 2)
    arrays["b2_columns"] = _np.ascontiguousarray(columns(arrays.pop("L2_ffn_b2")))
    arrays.update(shape_constants())
    nc = _bacc.Bacc("TRN2", target_bir_lowering=False, num_devices=1)
    args = {n: nc.dram_tensor(f"in_{n}", v.shape, _mybir.dt.from_np(v.dtype), kind="ExternalInput").ap()
            for n, v in arrays.items()}
    out = nc.dram_tensor("out_xT", arrays["xT"].shape, _mybir.dt.float32, kind="ExternalOutput").ap()
    program(nc, args, out, STOP)
    r = _run(nc, [{f"in_{n}": v for n, v in arrays.items()}], core_ids=[0])
    got = r.results[0]["out_xT"]
    return _np.ascontiguousarray(got.T).reshape(_np.asarray(inputs["x"]).shape)
```
